# Optimizing a Trainium2 kernel written in Bass

```python
import numpy as np
import jax
import jax.numpy as jnp

def _softmax(x, axis=-1):
    return jax.nn.softmax(x, axis=axis)

def _gelu(x):
    return jax.nn.gelu(x, approximate=True)

def _silu(x):
    return jax.nn.silu(x)

def _sigmoid(x):
    return jax.nn.sigmoid(x)

def _layernorm(x, axis=-1, eps=1e-05):
    m = jnp.mean(x, axis=axis, keepdims=True)
    v = jnp.var(x, axis=axis, keepdims=True)
    return (x - m) / jnp.sqrt(v + eps)

def _scatter_add(tgt, idx, src, axis=0):
    return tgt.at[idx].add(src)

def _segment_sum(src, seg, n):
    return jax.ops.segment_sum(src, seg, n)
kernel_name = 'mk_cond_resid_d2_seqx_r8_5a005d'

def setup_inputs(seed: int=0):
    np.random.seed(seed)
    _w = jnp.asarray

    def _rec_inputs():
        import jax
        import jax.numpy as jnp
        _rk = jax.random.key(seed)
        x = -1.394e-06 + 0.9999 * jax.random.normal(jax.random.fold_in(_rk, 1), (16, 128, 256), jnp.float32)
        _lenS = 128 - jax.random.randint(jax.random.fold_in(_rk, 7), (16,), 0, max(1, 128 // 4) + 1, jnp.int32)
        _lenS2 = 128 - jax.random.randint(jax.random.fold_in(_rk, 8), (16,), 0, max(1, 128 // 4) + 1, jnp.int32)
        cond_2048 = -0.00499425 + 1.0058 * jax.random.normal(jax.random.fold_in(_rk, 11), (16, 256), jnp.float32)
        return (x, cond_2048)
    x, cond_2048 = _rec_inputs()

    def _L0_cond_setup():
        import jax, jax.numpy as jnp
        import numpy as np
        B, T, D = (16, 128, 256)
        key = jax.random.key(seed)
        k0, k1, k2, k3 = jax.random.split(key, 4)
        scale = 1.0 / np.sqrt(D)
        return {'initial_state': jax.random.normal(k0, (B, D), jnp.float32), 'inputs': jax.random.normal(k1, (B, T, D), jnp.float32), 'W_ih': jax.random.normal(k2, (D, 3 * D), jnp.float32) * scale, 'W_hh': jax.random.normal(k3, (D, 3 * D), jnp.float32) * scale, 'b_ih': jnp.zeros((3 * D,), jnp.float32), 'b_hh': jnp.zeros((3 * D,), jnp.float32)}
    _L0_cond_all = _L0_cond_setup()
    _L0_cond_in = {k: v for k, v in _L0_cond_all.items() if k in ('W_ih', 'W_hh', 'b_ih', 'b_hh')}
    del _L0_cond_all

    def _L1_cond_setup():
        import jax, jax.numpy as jnp
        import numpy as np
        DIM = 256
        H = 16
        DH = 128
        INNER = H * DH
        MLP = 4 * DIM
        B, T = (2, 256)
        EPS = 1e-06

        def _ln(x):
            mu = jnp.mean(x, axis=-1, keepdims=True)
            var = jnp.var(x, axis=-1, keepdims=True)
            return (x - mu) * jax.lax.rsqrt(var + EPS)
        key = jax.random.key(seed)
        ks = jax.random.split(key, 12)
        s = 0.02
        return {'x': jax.random.normal(ks[0], (B, T, DIM), jnp.float32), 'timestep_embed': jax.random.normal(ks[1], (B, DIM), jnp.float32), 'ada_w': jax.random.normal(ks[2], (DIM, 6 * DIM), jnp.float32) * s, 'ada_b': jnp.zeros((6 * DIM,), jnp.float32), 'qkv_w': jax.random.normal(ks[3], (DIM, 3 * INNER), jnp.float32) * s, 'qkv_b': jnp.zeros((3 * INNER,), jnp.float32), 'out_w': jax.random.normal(ks[4], (INNER, DIM), jnp.float32) * s, 'out_b': jnp.zeros((DIM,), jnp.float32), 'ffn_w1': jax.random.normal(ks[5], (DIM, MLP), jnp.float32) * s, 'ffn_b1': jnp.zeros((MLP,), jnp.float32), 'ffn_w2': jax.random.normal(ks[6], (MLP, DIM), jnp.float32) * s, 'ffn_b2': jnp.zeros((DIM,), jnp.float32)}
    _L1_cond_all = _L1_cond_setup()
    _L1_cond_in = {k: v for k, v in _L1_cond_all.items() if k in ('ada_w', 'ada_b', 'qkv_w', 'qkv_b', 'out_w', 'out_b', 'ffn_w1', 'ffn_b1', 'ffn_w2', 'ffn_b2')}
    del _L1_cond_all
    return {'x': x, 'cond_2048': cond_2048, 'L0_cond_W_ih': _L0_cond_in['W_ih'], 'L0_cond_W_hh': _L0_cond_in['W_hh'], 'L0_cond_b_ih': _L0_cond_in['b_ih'], 'L0_cond_b_hh': _L0_cond_in['b_hh'], 'L1_cond_ada_w': _L1_cond_in['ada_w'], 'L1_cond_ada_b': _L1_cond_in['ada_b'], 'L1_cond_qkv_w': _L1_cond_in['qkv_w'], 'L1_cond_qkv_b': _L1_cond_in['qkv_b'], 'L1_cond_out_w': _L1_cond_in['out_w'], 'L1_cond_out_b': _L1_cond_in['out_b'], 'L1_cond_ffn_w1': _L1_cond_in['ffn_w1'], 'L1_cond_ffn_b1': _L1_cond_in['ffn_b1'], 'L1_cond_ffn_w2': _L1_cond_in['ffn_w2'], 'L1_cond_ffn_b2': _L1_cond_in['ffn_b2']}

def reference(x, cond_2048, L0_cond_W_ih, L0_cond_W_hh, L0_cond_b_ih, L0_cond_b_hh, L1_cond_ada_w, L1_cond_ada_b, L1_cond_qkv_w, L1_cond_qkv_b, L1_cond_out_w, L1_cond_out_b, L1_cond_ffn_w1, L1_cond_ffn_b1, L1_cond_ffn_w2, L1_cond_ffn_b2):
    import jax
    import jax.numpy as jnp

    def _L0_cond_ref(initial_state, inputs, W_ih, W_hh, b_ih, b_hh):
        import jax, jax.numpy as jnp
        import numpy as np
        B, T, D = (16, 128, 256)
        "ScanOverTime(GRU cell): sequential per-timestep module call with\n            dict-state passing; merge_dict_trees stacks the per-step\n            'state_predicted' tensors along axis=1 -> [B, T, D]."

        def cell(h, x):
            gi = x @ W_ih + b_ih
            gh = h @ W_hh + b_hh
            i_r, i_z, i_n = jnp.split(gi, 3, axis=-1)
            h_r, h_z, h_n = jnp.split(gh, 3, axis=-1)
            r = jax.nn.sigmoid(i_r + h_r)
            z = jax.nn.sigmoid(i_z + h_z)
            n = jnp.tanh(i_n + r * h_n)
            h_new = (1.0 - z) * n + z * h
            return (h_new, h_new)
        xs = jnp.swapaxes(inputs, 0, 1)
        _, hs = jax.lax.scan(cell, initial_state, xs)
        return jnp.swapaxes(hs, 0, 1)

    def _L1_cond_ref(x, timestep_embed, ada_w, ada_b, qkv_w, qkv_b, out_w, out_b, ffn_w1, ffn_b1, ffn_w2, ffn_b2):
        import jax, jax.numpy as jnp
        import numpy as np
        DIM = 256
        H = 16
        DH = 128
        INNER = H * DH
        MLP = 4 * DIM
        B, T = (2, 256)
        EPS = 1e-06

        def _ln(x):
            mu = jnp.mean(x, axis=-1, keepdims=True)
            var = jnp.var(x, axis=-1, keepdims=True)
            return (x - mu) * jax.lax.rsqrt(var + EPS)
        Bc, Tc, D = x.shape
        ada = (timestep_embed @ ada_w + ada_b)[:, None, :]
        shift1, scale1, gate1, shift2, scale2, gate2 = jnp.split(ada, 6, axis=-1)
        x1 = _ln(x) * (1.0 + scale1) + shift1
        qkv = (x1 @ qkv_w + qkv_b).reshape(Bc, Tc, 3, H, DH)
        q, k, v = (qkv[:, :, 0], qkv[:, :, 1], qkv[:, :, 2])
        scale = DH ** (-0.5)
        attn = jnp.einsum('bthd,bshd->bhts', q, k) * scale
        attn = jax.nn.softmax(attn, axis=-1)
        attn_out = jnp.einsum('bhts,bshd->bthd', attn, v).reshape(Bc, Tc, INNER)
        attn_out = attn_out @ out_w + out_b
        x = x + gate1 * attn_out
        x2 = _ln(x) * (1.0 + scale2) + shift2
        h = jax.nn.gelu(x2 @ ffn_w1 + ffn_b1, approximate=False)
        x = x + gate2 * (h @ ffn_w2 + ffn_b2)
        return x
    x = x + _L0_cond_ref(cond_2048, x, L0_cond_W_ih, L0_cond_W_hh, L0_cond_b_ih, L0_cond_b_hh)
    x = x + _L1_cond_ref(x, cond_2048, L1_cond_ada_w, L1_cond_ada_b, L1_cond_qkv_w, L1_cond_qkv_b, L1_cond_out_w, L1_cond_out_b, L1_cond_ffn_w1, L1_cond_ffn_b1, L1_cond_ffn_w2, L1_cond_ffn_b2)
    return x

_drawn_inputs = setup_inputs


def setup_inputs(seed=0):
    import zlib

    import numpy as np

    out = dict(_drawn_inputs(seed))
    spreads = {'L0_cond_b_ih': (0.0, 0.1),
     'L0_cond_b_hh': (0.0, 0.1),
     'L1_cond_ada_b': (0.0, 0.684),
     'L1_cond_qkv_b': (0.0, 0.519),
     'L1_cond_out_b': (0.0, 0.538),
     'L1_cond_ffn_b1': (0.0, 0.8),
     'L1_cond_ffn_b2': (0.0, 0.493)}
    factors = {'L1_cond_qkv_w': 3.415, 'L1_cond_ffn_w1': 3.03, 'L1_cond_ffn_w2': 2.818}
    for name, (base, spread) in spreads.items():
        noise = np.random.default_rng([zlib.crc32(name.encode()), seed]).standard_normal(out[name].shape)
        drawn = base * np.exp(spread * noise) if base else spread * noise
        out[name] = jnp.asarray(drawn.astype(out[name].dtype))
    for name, factor in factors.items():
        out[name] = (out[name] * factor).astype(out[name].dtype)
    return out
```

```python
import concourse.bass as bass
from concourse import mybir
from contextlib import ExitStack

P = 128
B, T, D = 16, 128, 256
KD = D // P
GATES = 3 * D
GM = GATES // P
H, DH = 16, 128
INNER = H * DH
MLP = 4 * D
FM = MLP // P
ADA = 6 * D // P
QUAD = 4
NG = B // QUAD
N = QUAD * T
CT = N // B
EPS = 1e-6
SCALE = DH ** -0.5
CH = 2048

BI, BH, BA, BQ = 0, GM, 2 * GM, 2 * GM + ADA
BO = BQ + 3 * H
B1 = BO + KD
B2 = B1 + FM
NB = B2 + KD
SH1, SC1, G1, SH2, SC2, G2 = (i * KD for i in range(6))


def build(nc, x, cond, W_ih, W_hh, b_ih, b_hh, ada_w, ada_b, qkv_w, qkv_b, out_w, out_b,
          f1_w, f1_b, f2_w, f2_b, out):
    f32, f16 = mybir.dt.float32, mybir.dt.float16
    ALU, ACT, AX = mybir.AluOpType, mybir.ActivationFunctionType, mybir.AxisListType
    ctx = ExitStack()
    with ctx:
        def sb(name, shape, dt=f32, scope=ctx):
            return scope.enter_context(nc.sbuf_tensor(name, shape, dt))

        def sem(name):
            return ctx.enter_context(nc.semaphore(name))

        ident = sb("ident", [P, P])
        ident16 = sb("ident16", [P, P], f16)
        w_hi = sb("w_hi", [P, 10 * CH], f16)
        w_lo = sb("w_lo", [P, 10 * CH], f16)
        bT = sb("bT", [P, NB])
        ada = sb("ada", [P, ADA, B])
        gbo = sb("gbo", [P, KD, B])
        gb2 = sb("gb2", [P, KD, B])
        xr = sb("xr", [P, KD, B, T])
        nhalf = sb("nhalf", [P, B])
        gru = ExitStack()
        stage = sb("stage", [P, 2, CH], f32, gru)
        hs = sb("hs", [P, KD, T + 1, B], f32, gru)
        xT = sb("xT", [P, KD, T, B], f32, gru)
        gi_hi = sb("gi_hi", [P, T, 4, B], f16, gru)
        gi_lo = sb("gi_lo", [P, T, 4, B], f16, gru)
        gin = sb("gin", [P, T, KD, B], f32, gru)
        whh_hi = sb("whh_hi", [P, KD, GATES], f16, gru)
        whh_lo = sb("whh_lo", [P, KD, GATES], f16, gru)
        bhn = sb("bhn", [P, 2, KD, B], f16, gru)
        bhn32 = sb("bhn32", [P, KD, B], f32, gru)
        brz = sb("brz", [P, 4], f32, gru)
        h_hi = sb("h_hi", [P, KD, B], f16, gru)
        h_lo = sb("h_lo", [P, KD, B], f16, gru)
        rg = sb("rg", [P, KD, B], f32, gru)
        zg = sb("zg", [P, KD, B], f32, gru)
        ng = sb("ng", [P, KD, B], f32, gru)
        rhn = sb("rhn", [P, KD, B], f32, gru)
        npre = sb("npre", [P, KD, B], f32, gru)
        hmn = sb("hmn", [P, KD, B], f32, gru)
        zhmn = sb("zhmn", [P, KD, B], f32, gru)
        pre = ExitStack()
        xin = xr[:, :, :, :].rearrange("p k b t -> p (k b t)").rearrange("p (b d) -> p b d", d=D)
        brow = sb("brow", [NB, P], f32, pre)
        crow = sb("crow", [B, D], f32, pre)
        adaw = stage[:, :, :].rearrange("p s c -> p (s c)")[:, 0:KD * 6 * D].rearrange("p (k c) -> p k c", k=KD)
        wg32 = gin[:, :, :, :].rearrange("p t k b -> p (t k b)")[:, 0:2 * KD * GATES].rearrange(
            "p (n k c) -> p n k c", n=2, k=KD)
        wih_hi = w_hi[:, KD * T * B:KD * (T * B + GATES)].rearrange("p (k c) -> p k c", k=KD)
        wih_lo = w_lo[:, KD * T * B:KD * (T * B + GATES)].rearrange("p (k c) -> p k c", k=KD)
        pre.close()
        xT_hi = w_hi[:, 0:KD * T * B].rearrange("p (k t b) -> p k t b", k=KD, t=T)
        xT_lo = w_lo[:, 0:KD * T * B].rearrange("p (k t b) -> p k t b", k=KD, t=T)
        gru.close()
        y_hi = sb("y_hi", [P, KD, B, T], f16)
        y_lo = sb("y_lo", [P, KD, B, T], f16)
        nat = sb("nat", [P, B, D])
        xr2 = sb("xr2", [P, KD, B, T])
        st6 = sb("st6", [P, B, 6])
        part = sb("part", [P, 3, B])
        mean = sb("mean", [P, B])
        msq = sb("msq", [P, B])
        mvar = sb("mvar", [P, B])
        rstd = sb("rstd", [P, B])
        veps = sb("veps", [P, B])
        tin = sb("tin", [P, 2, KD, T])
        xn = sb("xn", [P, 2, D])
        yf = sb("yf", [P, 2, KD, T])
        qT_hi = sb("qT_hi", [P, N], f16)
        qT_lo = sb("qT_lo", [P, N], f16)
        kT_hi = sb("kT_hi", [P, N], f16)
        kT_lo = sb("kT_lo", [P, N], f16)
        v_hi = sb("v_hi", [P, 2, N], f16)
        v_lo = sb("v_lo", [P, 2, N], f16)
        pT_hi = sb("pT_hi", [P, N], f16)
        pT_lo = sb("pT_lo", [P, N], f16)
        aT_hi = sb("aT_hi", [P, N], f16)
        aT_lo = sb("aT_lo", [P, N], f16)
        prob = sb("prob", [P, QUAD, T])
        pn = sb("pn", [P, QUAD, T])
        mx = sb("mx", [P, QUAD])
        nmx = sb("nmx", [P, QUAD])
        den = sb("den", [P, QUAD])
        rden = sb("rden", [P, QUAD])
        gated = sb("gated", [P, KD, QUAD, T])
        hf = sb("hf", [P, 2, N])
        hid_hi = sb("hid_hi", [P, 2, N], f16)
        hid_lo = sb("hid_lo", [P, 2, N], f16)
        yT = sb("yT", [P, KD, QUAD, T])
        ynat = sb("ynat", [P, 2, D])

        bank = [ctx.enter_context(nc.psum_tensor(f"bank{i}", [P, 512], f32)) for i in range(8)]

        wq_hi = w_hi[:, 0:6 * CH].rearrange("p (k c) -> p k c", k=KD)
        wq_lo = w_lo[:, 0:6 * CH].rearrange("p (k c) -> p k c", k=KD)
        wo_hi = w_hi[:, 6 * CH:8 * CH]
        wo_lo = w_lo[:, 6 * CH:8 * CH]
        w1_hi = w_hi[:, 8 * CH:9 * CH].rearrange("p (k c) -> p k c", k=KD)
        w1_lo = w_lo[:, 8 * CH:9 * CH].rearrange("p (k c) -> p k c", k=KD)
        w2_hi = w_hi[:, 9 * CH:10 * CH].rearrange("p (m c) -> p m c", m=FM)
        w2_lo = w_lo[:, 9 * CH:10 * CH].rearrange("p (m c) -> p m c", m=FM)


        def sems(names):
            return [sem(n) for n in names.split()]

        stage_in = sems("stage_in0 stage_in1")
        (rows_in, gatew_in, x_in, adaw_in, ident0, ident_ok, const_ok, small_T, small_sb, state_ok, xt_T, xt_hi, xt_32,
         xt_lo, wg_hi, wg_lo, gi_mm, gi_h, gi_done, ada_mm, ada_add, ada_ok, brz_ok, bhn_a, bhn_b, bhn_ok,
         chunk_hi, chunk_lo) = sems(
             "rows_in gatew_in x_in adaw_in ident0 ident_ok const_ok small_T small_sb state_ok xt_T xt_hi xt_32 "
             "xt_lo wg_hi wg_lo gi_mm gi_h gi_done ada_mm ada_add ada_ok brz_ok bhn_a bhn_b bhn_ok "
             "chunk_hi chunk_lo")
        (r_mm, hn_mm, z_mm, r_ok, z_ok, n_ok, rhn_ok, npre_ok, hmn_ok, zhmn_ok, hhi_ok, h32_ok, hlo_ok) = sems(
            "r_mm hn_mm z_mm r_ok z_ok n_ok rhn_ok npre_ok hmn_ok zhmn_ok hhi_ok h32_ok hlo_ok")
        (xr_ok, ln_in, ln_ag, ln_T, ln_nat, ln_st, ln_ve, ln_rstd, ln_xn, ln_B, ln_y, ln_hi, ln_lo) = sems(
            "xr_ok ln_in ln_ag ln_T ln_nat ln_st ln_ve ln_rstd ln_xn ln_B ln_y ln_hi ln_lo")
        (q_mm, k_mm, v_mm, s_mm, p_T, a_mm, o_mm, q_h, k_h, v_h, q_l, k_l, v_l, s_mx, s_nm, s_exp, s_rd, s_pn,
         p_h, p_l, a_h, a_l, o_gated, o_res) = sems(
             "q_mm k_mm v_mm s_mm p_T a_mm o_mm q_h k_h v_h q_l k_l v_l s_mx s_nm s_exp s_rd s_pn "
             "p_h p_l a_h a_l o_gated o_res")
        (f_up, f_gelu, f_hi, f_lo, f_down, f_gated, f_sum, f_out, y_T, y_nat) = sems(
            "f_up f_gelu f_hi f_lo f_down f_gated f_sum f_out y_T y_nat")
        y_out = sems("y_out0 y_out1")

        block = ctx.enter_context(nc.Block())

        qkv_v = qkv_w.rearrange("(k p) c -> p k c", p=P)
        wo_v = out_w.rearrange("(h p) d -> p h d", p=P)
        chunks = [qkv_v[:, c // 3, (c % 3) * CH:(c % 3 + 1) * CH] for c in range(6)]
        chunks += [wo_v[:, 0:8, :], wo_v[:, 8:16, :], f1_w.rearrange("(k p) c -> p k c", p=P),
                   f2_w.rearrange("(m p) d -> p m d", p=P)]
        NC = len(chunks)

        def cols(at, n):
            return slice(at, at + n) if isinstance(at, int) else bass.ds(at, n)

        @block.sync
        def _(sp):
            for at, src, n in ((BI, b_ih, GM), (BH, b_hh, GM), (BA, ada_b, ADA), (BQ, qkv_b, 3 * H), (BO, out_b, KD),
                               (B1, f1_b, FM), (B2, f2_b, KD)):
                sp.dma_start(brow[at:at + n, :], src.rearrange("(n p) -> n p", p=P)).then_inc(rows_in, 16)
            sp.dma_start(crow[:, :], cond).then_inc(rows_in, 16)
            for n, w in enumerate((W_ih, W_hh)):
                sp.dma_start(wg32[:, n, :, :], w.rearrange("(k p) c -> p k c", p=P)).then_inc(gatew_in, 16)
            sp.dma_start(xin, x.rearrange("b t d -> t b d")).then_inc(x_in, 16)
            sp.dma_start(adaw, ada_w.rearrange("(k p) c -> p k c", p=P)).then_inc(adaw_in, 16)
            for c, src in enumerate(chunks):
                if c == 0:
                    sp.wait_ge(ada_mm, 1)
                if c >= 2:
                    sp.wait_ge(chunk_lo, c - 1)
                dst = stage[:, c % 2, :]
                sp.dma_start(dst if c < 6 else dst.rearrange("p (a b) -> p a b", a=src.shape[1]),
                             src).then_inc(stage_in[c % 2], 16)
            with sp.Fori(0, B - 1, 2) as b:
                for u in (0, 1):
                    sp.wait_ge(y_nat, b + u + 1)
                    sp.dma_start(out[b + u], ynat[:, u, :]).then_inc(y_out[u], 16)
            for u in (0, 1):
                sp.wait_ge(y_out[u], 16 * B // 2)

        @block.gpsimd
        def _(pool):
            nc.gpsimd.memset(ident[:, :], 0.0).then_inc(ident0, 1)
            pool.wait_ge(ident0, 1)
            nc.gpsimd.affine_select(out=ident[:, :], in_=ident[:, :], compare_op=ALU.not_equal, fill=1.0, base=0,
                                    pattern=[[-1, P]], channel_multiplier=1).then_inc(ident_ok, 1)
            pool.wait_ge(ident_ok, 1)
            nc.gpsimd.tensor_copy(ident16[:, :], ident[:, :]).then_inc(const_ok, 1)
            nc.gpsimd.memset(nhalf[:, :], -0.5).then_inc(const_ok, 1)
            pool.wait_ge(gi_mm, NG * GM)
            for c in range(NC):
                at = slice(c * CH, (c + 1) * CH)
                pool.wait_ge(stage_in[c % 2], 16 * (c // 2 + 1))
                nc.gpsimd.tensor_copy(w_hi[:, at], stage[:, c % 2, :]).then_inc(chunk_hi, 1)
                pool.wait_ge(chunk_hi, c + 1)
                nc.gpsimd.tensor_tensor(w_lo[:, at], stage[:, c % 2, :], w_hi[:, at],
                                        ALU.subtract).then_inc(chunk_lo, 1)
            pool.wait_ge(const_ok, 2)
            for n in (0, 1):
                pool.wait_ge(o_res if n else xr_ok, NG if n else KD)
                with pool.Fori(0, B - 1, 2) as b:
                    for u in (0, 1):
                        pool.wait_ge(ln_T, b + n * B)
                        nc.gpsimd.tensor_copy(tin[:, u, :, :], (xr2 if n else xr)[:, :, b + u, :]).then_inc(ln_in, 1)
                pool.wait_ge(ln_ve, n + 1)
                nc.gpsimd.tensor_tensor(rstd[:, :], veps[:, :], nhalf[:, :], ALU.pow).then_inc(ln_rstd, 1)
                with pool.Fori(0, B - 1, 2) as b:
                    for u in (0, 1):
                        pool.wait_ge(ln_hi, b + (n * B + u + 1))
                        nc.gpsimd.tensor_tensor(y_lo[:, :, b + u, :], yf[:, u, :, :], y_hi[:, :, b + u, :],
                                                ALU.subtract).then_inc(ln_lo, 1)

        @block.tensor
        def _(pe):
            def product(ps, w, a, start, stop):
                mm = nc.tensor.matmul
                mm(ps, w[0], a[0], start=start, stop=False, skip_group_check=True)
                mm(ps, w[1], a[0], start=False, stop=False, skip_group_check=True)
                return mm(ps, w[0], a[1], start=False, stop=stop, skip_group_check=True)

            pe.wait_ge(ident_ok, 1)
            pe.wait_ge(rows_in, 16 * 8)
            nc.tensor.transpose(bank[0][:, 0:NB], brow[:, :], ident[0:NB, 0:NB])
            for k in range(KD):
                mm = nc.tensor.transpose(bank[0][:, P + k * B:P + (k + 1) * B], crow[:, k * P:(k + 1) * P],
                                         ident[0:B, 0:B])
            mm.then_inc(small_T, 1)
            pe.wait_ge(x_in, 16)
            for n in range(NG * KD):
                g, k = n // KD, n % KD
                if n >= 4:
                    pe.wait_ge(xt_32, n - 3)
                for j in range(QUAD):
                    mm = nc.tensor.transpose(bank[1 + n % 4][:, j * T:(j + 1) * T],
                                             xin[:, QUAD * g + j, k * P:(k + 1) * P], ident[:, :])
                mm.then_inc(xt_T, 1)
            pe.wait_ge(adaw_in, 16)
            pe.wait_ge(state_ok, 1)
            for m in range(ADA):
                for k in range(KD):
                    mm = nc.tensor.matmul(bank[5][:, m * B:(m + 1) * B], adaw[:, k, m * P:(m + 1) * P],
                                          hs[:, k, 0, :], start=(k == 0), stop=(k == KD - 1))
            mm.then_inc(ada_mm, 1)
            pe.wait_ge(xt_lo, NG * KD)
            pe.wait_ge(wg_lo, 1)
            for n in range(NG * GM):
                c, m = n // GM, n % GM
                if n >= 4:
                    pe.wait_ge(gi_done, n - 3)
                for k in range(KD):
                    w, tt = slice(m * P, (m + 1) * P), slice(c * CT, (c + 1) * CT)
                    mm = product(bank[1 + n % 4][:, :], (wih_hi[:, k, w], wih_lo[:, k, w]),
                                 (xT_hi[:, k, tt, :], xT_lo[:, k, tt, :]), k == 0, k == KD - 1)
                mm.then_inc(gi_mm, 1)
            pe.wait_ge(gi_done, NG * GM)
            pe.wait_ge(bhn_ok, 1)
            pe.wait_ge(const_ok, 1)
            pe.wait_ge(wg_lo, 2)
            rb, hb, zb = bank[0], bank[6], bank[7]

            with pe.Fori(0, T) as t:
                t1 = t + 1

                def gate(ps, m0, done):
                    for m in (0, 1):
                        for k in range(KD):
                            w = slice((m0 + m) * P, (m0 + m + 1) * P)
                            for half in (whh_hi, whh_lo):
                                nc.tensor.matmul(ps[:, m * B:(m + 1) * B], half[:, k, w], h_hi[:, k, :], start=False,
                                                 stop=False, skip_group_check=True)
                    if done is r_mm:
                        pe.wait_ge(hlo_ok, t1)
                    for m in (0, 1):
                        for k in range(KD):
                            w = slice((m0 + m) * P, (m0 + m + 1) * P)
                            mm = nc.tensor.matmul(ps[:, m * B:(m + 1) * B], whh_hi[:, k, w], h_lo[:, k, :],
                                                  start=False, stop=True, skip_group_check=True)
                    mm.then_inc(done, 1)

                pe.wait_ge(z_ok, t)
                pe.wait_ge(rhn_ok, t)
                for half, first in ((gi_hi, True), (gi_lo, False)):
                    nc.tensor.matmul(rb[:, 0:KD * B], ident16[:, :], half[:, t, 0:2, :], start=first, stop=False,
                                     skip_group_check=True)
                    nc.tensor.matmul(zb[:, 0:KD * B], ident16[:, :], half[:, t, 2:4, :], start=first, stop=False,
                                     skip_group_check=True)
                for i in (0, 1):
                    nc.tensor.matmul(hb[:, 0:KD * B], ident16[:, :], bhn[:, i, :, :], start=(i == 0), stop=False,
                                     skip_group_check=True)
                pe.wait_ge(hhi_ok, t1)
                gate(rb, 0, r_mm)
                gate(hb, 4, hn_mm)
                gate(zb, 2, z_mm)

            def layer_norm(n):
                with pe.Fori(0, B - 1, 2) as b:
                    for u in (0, 1):
                        pe.wait_ge(ln_nat, b + n * B)
                        pe.wait_ge(ln_in, b + (n * B + u + 1))
                        for k in range(KD):
                            mm = nc.tensor.transpose(bank[u][:, k * P:(k + 1) * P], tin[:, u, k, :], ident[:, :])
                        mm.then_inc(ln_T, 1)
                with pe.Fori(0, B - 1, 2) as b:
                    for u in (0, 1):
                        pe.wait_ge(ln_xn, b + (n * B + u + 1))
                        pe.wait_ge(ln_y, b + n * B)
                        for k in range(KD):
                            mm = nc.tensor.transpose(bank[2 + u][:, k * T:(k + 1) * T],
                                                     xn[:, u, k * P:(k + 1) * P], ident[:, :])
                        mm.then_inc(ln_B, 1)

            layer_norm(0)
            pe.wait_ge(ln_lo, B)
            pe.wait_ge(chunk_lo, NC)

            def project_out(g, i, static):
                pe.wait_ge(a_l, g * H + (i - 1))
                if static and i == 2:
                    pe.wait_ge(o_gated, g)
                for k in range(KD):
                    w = cols((i - 2) * D + k * P, P)
                    mm = product(bank[6 + k][:, :], (wo_hi[:, w], wo_lo[:, w]), (aT_hi[:, :], aT_lo[:, :]),
                                 static and i == 2, static and i == H + 1)
                if static and i == H + 1:
                    mm.then_inc(o_mm, 1)

            def step(g, i, u, static):
                new, old, add = (not static or i < H), (not static or 1 <= i <= H), (not static or i >= 2)
                done = g * H + i
                quad = cols(g * QUAD, QUAD)
                if new:
                    pe.wait_ge(q_l, done)
                    for k in range(KD):
                        w = cols(i * DH, DH)
                        mm = product(bank[0][:, :], (wq_hi[:, k, w], wq_lo[:, k, w]),
                                     (y_hi[:, k, quad, :], y_lo[:, k, quad, :]), k == 0, k == KD - 1)
                    mm.then_inc(q_mm, 1)
                if add:
                    project_out(g, i, static)
                if new:
                    pe.wait_ge(k_l, done)
                    for k in range(KD):
                        w = cols((i + H) * DH, DH)
                        mm = product(bank[1][:, :], (wq_hi[:, k, w], wq_lo[:, k, w]),
                                     (y_hi[:, k, quad, :], y_lo[:, k, quad, :]), k == 0, k == KD - 1)
                    mm.then_inc(k_mm, 1)
                if old:
                    pe.wait_ge(s_pn, done)
                    for j in range(QUAD):
                        mm = nc.tensor.transpose(bank[4][:, j * T:(j + 1) * T], pn[:, j, :], ident[:, :])
                    mm.then_inc(p_T, 1)
                if new:
                    pe.wait_ge(v_l, done)
                    w = cols((i + 2 * H) * DH, DH)
                    for j in range(QUAD):
                        for k in range(KD):
                            mm = product(bank[2][:, j * DH:(j + 1) * DH],
                                         (y_hi[:, k, g * QUAD + j, :], y_lo[:, k, g * QUAD + j, :]),
                                         (wq_hi[:, k, w], wq_lo[:, k, w]), j == 0 and k == 0, k == KD - 1)
                    mm.then_inc(v_mm, 1)
                if old:
                    pe.wait_ge(p_l, done)
                    for j in range(QUAD):
                        c = slice(j * T, (j + 1) * T)
                        mm = product(bank[5][:, c], (v_hi[:, 1 - u, c], v_lo[:, 1 - u, c]), (pT_hi[:, c], pT_lo[:, c]),
                                     j == 0, True)
                    mm.then_inc(a_mm, 1)
                if new:
                    pe.wait_ge(q_l, done + 1)
                    pe.wait_ge(k_l, done + 1)
                    pe.wait_ge(s_exp, done)
                    for j in range(QUAD):
                        c = slice(j * T, (j + 1) * T)
                        mm = product(bank[3][:, c], (qT_hi[:, c], qT_lo[:, c]), (kT_hi[:, c], kT_lo[:, c]),
                                     j == 0, True)
                    mm.then_inc(s_mm, 1)

            with pe.Fori(0, NG) as g:
                for i in range(4):
                    step(g, i, i % 2, True)
                with pe.Fori(4, H - 1, 2) as i:
                    for u in (0, 1):
                        step(g, i + u, u, False)
                for i in (H, H + 1):
                    step(g, i, i % 2, True)

            layer_norm(1)
            pe.wait_ge(ln_lo, 2 * B)
            with pe.Fori(0, NG) as g:
                quad = cols(g * QUAD, QUAD)
                for m in range(FM + 1):
                    if m < FM:
                        pe.wait_ge(f_gelu, g * FM + max(m - 1, 0))
                        w = slice(m * P, (m + 1) * P)
                        for k in range(KD):
                            mm = product(bank[m % 2][:, :], (w1_hi[:, k, w], w1_lo[:, k, w]),
                                         (y_hi[:, k, quad, :], y_lo[:, k, quad, :]), k == 0, k == KD - 1)
                        mm.then_inc(f_up, 1)
                    if m > 0:
                        pe.wait_ge(f_lo, g * FM + m)
                        if m == 1:
                            pe.wait_ge(f_gated, g)
                        for k in range(KD):
                            w, a = slice(k * P, (k + 1) * P), (m - 1) % 2
                            mm = product(bank[4 + k][:, :], (w2_hi[:, m - 1, w], w2_lo[:, m - 1, w]),
                                         (hid_hi[:, a, :], hid_lo[:, a, :]), m == 1, m == FM)
                        mm.then_inc(f_down, 1)
                pe.wait_ge(f_out, g + 1)
                for j in range(QUAD):
                    pe.wait_ge(y_nat, g * QUAD + max(j - 1, 0))
                    for k in range(KD):
                        mm = nc.tensor.transpose(bank[2 + j % 2][:, k * P:(k + 1) * P], yT[:, k, j, :], ident[:, :])
                    mm.then_inc(y_T, 1)

        @block.scalar
        def _(act):
            copy, ident_f = ACT.Copy, ACT.Identity
            act.wait_ge(gatew_in, 32)
            nc.scalar.activation(whh_hi[:, :, :], wg32[:, 1, :, :], copy).then_inc(wg_hi, 1)
            nc.scalar.activation(wih_hi[:, :, :], wg32[:, 0, :, :], copy).then_inc(wg_hi, 1)
            for n in range(NG * KD):
                g, k = n // KD, n % KD
                act.wait_ge(xt_hi, n + 1)
                nc.scalar.activation(xT[:, k, :, QUAD * g:QUAD * (g + 1)].rearrange("p t b -> p b t"),
                                     bank[1 + n % 4][:, :].rearrange("p (b t) -> p b t", b=QUAD),
                                     copy).then_inc(xt_32, 1)
            act.wait_ge(brz_ok, 1)
            for c in range(NG):
                for m in range(4):
                    n = c * GM + m
                    act.wait_ge(gi_mm, n + 1)
                    nc.scalar.activation(gi_hi[:, c * CT:(c + 1) * CT, m, :],
                                         bank[1 + n % 4][:, :].rearrange("p (t b) -> p t b", b=B),
                                         ident_f, bias=brz[:, m:m + 1]).then_inc(gi_h, 1)
            with act.Fori(0, T) as t:
                t1 = t + 1
                act.wait_ge(r_mm, t1)
                nc.scalar.activation(rg[:, :, :], bank[0][:, 0:KD * B], ACT.Sigmoid).then_inc(r_ok, 1)
                act.wait_ge(npre_ok, t1)
                nc.scalar.activation(ng[:, :, :], npre[:, :, :], ACT.Tanh).then_inc(n_ok, 1)
                act.wait_ge(z_mm, t1)
                nc.scalar.activation(zg[:, :, :], bank[7][:, 0:KD * B], ACT.Sigmoid).then_inc(z_ok, 1)

            def layer_norm(n):
                with act.Fori(0, B - 1, 2) as b:
                    for u in (0, 1):
                        act.wait_ge(ln_T, b + (n * B + u + 1))
                        nc.scalar.activation(nat[:, b + u, :], bank[u][:, 0:D], copy).then_inc(ln_nat, 1)
                with act.Fori(0, B - 1, 2) as b:
                    for u in (0, 1):
                        act.wait_ge(ln_y, b + (n * B + u + 1))
                        nc.scalar.activation(y_hi[:, :, b + u, :], yf[:, u, :, :], copy).then_inc(ln_hi, 1)

            def step(g, i, u, static):
                new, old = (not static or i < H), (not static or 1 <= i <= H)
                done = g * H + i
                if old:
                    act.wait_ge(s_nm, done)
                    act.wait_ge(s_pn, done - 1)
                    for j in range(QUAD):
                        mm = nc.scalar.activation(prob[:, j, :], bank[3][:, j * T:(j + 1) * T], ACT.Exp,
                                                  bias=nmx[:, j:j + 1], scale=SCALE, accum_out=den[:, j:j + 1])
                    mm.then_inc(s_exp, 1)
                if new:
                    act.wait_ge(q_mm, done + 1)
                    act.wait_ge(s_mm, done)
                    nc.scalar.activation(qT_hi[:, :], bank[0][:, :], ident_f,
                                         bias=bT[:, cols(i + BQ, 1)]).then_inc(q_h, 1)
                    act.wait_ge(k_mm, done + 1)
                    nc.scalar.activation(kT_hi[:, :], bank[1][:, :], ident_f,
                                         bias=bT[:, cols(i + BQ + H, 1)]).then_inc(k_h, 1)
                if old:
                    act.wait_ge(p_T, done)
                    nc.scalar.activation(pT_hi[:, :], bank[4][:, :], copy).then_inc(p_h, 1)
                if new:
                    act.wait_ge(v_mm, done + 1)
                    nc.scalar.activation(v_hi[:, u, :], bank[2][:, :], copy).then_inc(v_h, 1)
                if old:
                    act.wait_ge(a_mm, done)
                    nc.scalar.activation(aT_hi[:, :], bank[5][:, :], ident_f,
                                         bias=bT[:, cols(i + BQ + 2 * H - 1, 1)]).then_inc(a_h, 1)

            def gate(g, base, bias, gate_tile, free):
                for k in range(KD):
                    for j in range(QUAD):
                        b = g * QUAD + j
                        mm = nc.scalar.activation(gated[:, k, j, :], bank[base + k][:, j * T:(j + 1) * T], ident_f,
                                                  bias=bias[:, k, cols(b, 1)], scale=ada[:, gate_tile + k, cols(b, 1)])
                return mm

            layer_norm(0)
            with act.Fori(0, NG) as g:
                for i in range(4):
                    step(g, i, i % 2, True)
                with act.Fori(4, H - 1, 2) as i:
                    for u in (0, 1):
                        step(g, i + u, u, False)
                step(g, H, 0, True)
                act.wait_ge(o_mm, g + 1)
                act.wait_ge(o_res, g)
                gate(g, 6, gbo, G1, o_res).then_inc(o_gated, 1)
            layer_norm(1)
            with act.Fori(0, NG) as g:
                for m in range(FM):
                    last = g * FM + max(m - 1, 0)
                    act.wait_ge(f_up, g * FM + (m + 1))
                    act.wait_ge(f_lo, last)
                    nc.scalar.activation(hf[:, m % 2, :], bank[m % 2][:, :], ACT.Gelu,
                                         bias=bT[:, B1 + m:B1 + m + 1]).then_inc(f_gelu, 1)
                    act.wait_ge(f_gelu, g * FM + (m + 1))
                    act.wait_ge(f_down, last)
                    nc.scalar.activation(hid_hi[:, m % 2, :], hf[:, m % 2, :], copy).then_inc(f_hi, 1)
                act.wait_ge(f_down, g * FM + FM)
                act.wait_ge(f_sum, g)
                gate(g, 4, gb2, G2, f_sum).then_inc(f_gated, 1)
                for j in range(QUAD):
                    act.wait_ge(y_T, g * QUAD + (j + 1))
                    if j >= 2:
                        act.wait_ge(y_out[j % 2], g * 32 + 16 * (j // 2))
                    else:
                        act.wait_ge(y_out[j % 2], g * 32)
                    nc.scalar.activation(ynat[:, j % 2, :], bank[2 + j % 2][:, 0:D], copy).then_inc(y_nat, 1)

        @block.vector
        def _(dve):
            tt, ts, stt = nc.vector.tensor_tensor, nc.vector.tensor_scalar, nc.vector.scalar_tensor_tensor
            dve.wait_ge(small_T, 1)
            nc.vector.tensor_copy(bT[:, :], bank[0][:, 0:NB]).then_inc(small_sb, 1)
            nc.vector.tensor_copy(hs[:, :, 0, :], bank[0][:, P:P + KD * B].rearrange("p (k b) -> p k b", k=KD)
                                  ).then_inc(state_ok, 1)
            dve.wait_ge(state_ok, 1)
            nc.vector.tensor_copy(h_hi[:, :, :], hs[:, :, 0, :]).then_inc(hhi_ok, 1)
            dve.wait_ge(hhi_ok, 1)
            tt(h_lo[:, :, :], hs[:, :, 0, :], h_hi[:, :, :], ALU.subtract).then_inc(hlo_ok, 1)
            dve.wait_ge(small_sb, 1)
            tt(brz[:, :], bT[:, BI:BI + 4], bT[:, BH:BH + 4], ALU.add).then_inc(brz_ok, 1)
            nc.vector.tensor_copy(bhn32[:, :, :], bT[:, BH + 4:BH + 6].unsqueeze(2).broadcast_to([P, KD, B])
                                  ).then_inc(bhn_a, 1)
            dve.wait_ge(bhn_a, 1)
            nc.vector.tensor_copy(bhn[:, 0, :, :], bhn32[:, :, :]).then_inc(bhn_b, 1)
            dve.wait_ge(bhn_b, 1)
            tt(bhn[:, 1, :, :], bhn32[:, :, :], bhn[:, 0, :, :], ALU.subtract).then_inc(bhn_ok, 1)
            for n, (hi, lo) in enumerate(((whh_hi, whh_lo), (wih_hi, wih_lo))):
                dve.wait_ge(wg_hi, n + 1)
                tt(lo[:, :, :], wg32[:, 1 - n, :, :], hi[:, :, :], ALU.subtract).then_inc(wg_lo, 1)

            def x_lo(n):
                q, k = slice(QUAD * (n // KD), QUAD * (n // KD + 1)), n % KD
                dve.wait_ge(xt_32, n + 1)
                tt(xT_lo[:, k, :, q], xT[:, k, :, q], xT_hi[:, k, :, q], ALU.subtract).then_inc(xt_lo, 1)

            for n in range(NG * KD):
                g, k = n // KD, n % KD
                dve.wait_ge(xt_T, n + 1)
                nc.vector.tensor_copy(xT_hi[:, k, :, QUAD * g:QUAD * (g + 1)].rearrange("p t b -> p b t"),
                                      bank[1 + n % 4][:, :].rearrange("p (b t) -> p b t", b=QUAD)).then_inc(xt_hi, 1)
                if n >= 1:
                    x_lo(n - 1)
            x_lo(NG * KD - 1)
            dve.wait_ge(ada_mm, 1)
            tt(ada[:, :, :], bank[5][:, 0:ADA * B].rearrange("p (m b) -> p m b", b=B),
               bT[:, BA:BA + ADA].unsqueeze(2).broadcast_to([P, ADA, B]), ALU.add).then_inc(ada_add, 1)
            dve.wait_ge(ada_add, 1)
            for sc in (SC1, SC2):
                nc.vector.tensor_scalar_add(ada[:, sc:sc + KD, :], ada[:, sc:sc + KD, :], 1.0).then_inc(ada_ok, 1)
            for dst, gate_tile, bias in ((gbo, G1, BO), (gb2, G2, B2)):
                tt(dst[:, :, :], ada[:, gate_tile:gate_tile + KD, :],
                   bT[:, bias:bias + KD].unsqueeze(2).broadcast_to([P, KD, B]), ALU.mult).then_inc(ada_ok, 1)
            for c in range(NG):
                for m in range(GM):
                    n = c * GM + m
                    ps = bank[1 + n % 4][:, :].rearrange("p (t b) -> p t b", b=B)
                    tc = slice(c * CT, (c + 1) * CT)
                    if m < 4:
                        dve.wait_ge(gi_h, c * 4 + m + 1)
                        stt(gi_lo[:, tc, m, :], ps, brz[:, m:m + 1], gi_hi[:, tc, m, :], ALU.add,
                            ALU.subtract).then_inc(gi_done, 1)
                    else:
                        dve.wait_ge(gi_mm, n + 1)
                        ts(gin[:, tc, m - 4, :], ps, bT[:, BI + m:BI + m + 1], None, ALU.add).then_inc(gi_done, 1)
            with dve.Fori(0, T) as t:
                t1 = t + 1
                dve.wait_ge(r_ok, t1)
                dve.wait_ge(hn_mm, t1)
                tt(rhn[:, :, :], rg[:, :, :], bank[6][:, 0:KD * B].rearrange("p (k b) -> p k b", k=KD),
                   ALU.mult).then_inc(rhn_ok, 1)
                dve.wait_ge(rhn_ok, t1)
                tt(npre[:, :, :], rhn[:, :, :], gin[:, t, :, :], ALU.add).then_inc(npre_ok, 1)
                dve.wait_ge(n_ok, t1)
                tt(hmn[:, :, :], hs[:, :, t, :], ng[:, :, :], ALU.subtract).then_inc(hmn_ok, 1)
                dve.wait_ge(hmn_ok, t1)
                dve.wait_ge(z_ok, t1)
                tt(zhmn[:, :, :], zg[:, :, :], hmn[:, :, :], ALU.mult).then_inc(zhmn_ok, 1)
                dve.wait_ge(zhmn_ok, t1)
                tt(h_hi[:, :, :], ng[:, :, :], zhmn[:, :, :], ALU.add).then_inc(hhi_ok, 1)
                tt(hs[:, :, t1, :], ng[:, :, :], zhmn[:, :, :], ALU.add).then_inc(h32_ok, 1)
                dve.wait_ge(hhi_ok, t + 2)
                dve.wait_ge(h32_ok, t1)
                tt(h_lo[:, :, :], hs[:, :, t1, :], h_hi[:, :, :], ALU.subtract).then_inc(hlo_ok, 1)
            for k in range(KD):
                tt(xr[:, k, :, :], xT[:, k, :, :].rearrange("p t b -> p b t"),
                   hs[:, k, 1:T + 1, :].rearrange("p t b -> p b t"), ALU.add).then_inc(xr_ok, 1)

            def layer_norm(n, shift, scale):
                with dve.Fori(0, B - 1, 2) as b:
                    for u in (0, 1):
                        dve.wait_ge(ln_nat, b + (n * B + u + 1))
                        nc.vector.bn_stats(st6[:, b + u, :], nat[:, b + u, :]).then_inc(ln_st, 1)
                dve.wait_ge(ln_st, (n + 1) * B)
                even_mean, even_m2, odd_mean, odd_m2 = (st6[:, :, i] for i in (1, 2, 4, 5))
                tt(part[:, 0, :], even_mean, odd_mean, ALU.add).then_inc(ln_ag, 1)
                tt(part[:, 1, :], even_mean, odd_mean, ALU.subtract).then_inc(ln_ag, 1)
                tt(part[:, 2, :], even_m2, odd_m2, ALU.add).then_inc(ln_ag, 1)
                dve.wait_ge(ln_ag, n * 6 + 3)
                ts(mean[:, :], part[:, 0, :], 0.5, None, ALU.mult).then_inc(ln_ag, 1)
                stt(msq[:, :], part[:, 1, :], 0.25, part[:, 1, :], ALU.mult, ALU.mult).then_inc(ln_ag, 1)
                ts(mvar[:, :], part[:, 2, :], 1.0 / D, EPS, ALU.mult, ALU.add).then_inc(ln_ag, 1)
                dve.wait_ge(ln_ag, n * 6 + 6)
                tt(veps[:, :], msq[:, :], mvar[:, :], ALU.add).then_inc(ln_ve, 1)
                dve.wait_ge(ln_rstd, n + 1)
                with dve.Fori(0, B - 1, 2) as b:
                    dve.wait_ge(ln_B, b + n * B)
                    for u in (0, 1):
                        ts(xn[:, u, :], nat[:, b + u, :], mean[:, cols(b + u, 1)], rstd[:, cols(b + u, 1)], ALU.subtract,
                           ALU.mult).then_inc(ln_xn, 1)
                    for u in (0, 1):
                        dve.wait_ge(ln_B, b + (n * B + u + 1))
                        dve.wait_ge(ln_lo, b + n * B)
                        for k in range(KD):
                            op = ts(yf[:, u, k, :], bank[2 + u][:, k * T:(k + 1) * T],
                                    ada[:, scale + k, cols(b + u, 1)], ada[:, shift + k, cols(b + u, 1)], ALU.mult,
                                    ALU.add)
                        op.then_inc(ln_y, 1)

            def step(g, i, u, static):
                new, old = (not static or i < H), (not static or 1 <= i <= H)
                done = g * H + i
                if old:
                    dve.wait_ge(s_mm, done)
                    nc.vector.reduce_max(mx[:, :], bank[3][:, :].rearrange("p (j s) -> p j s", j=QUAD),
                                         AX.X).then_inc(s_mx, 1)
                    dve.wait_ge(s_mx, done)
                    nc.vector.tensor_scalar_mul(nmx[:, :], mx[:, :], -SCALE).then_inc(s_nm, 1)
                if new:
                    dve.wait_ge(q_h, done + 1)
                    stt(qT_lo[:, :], bank[0][:, :], bT[:, cols(i + BQ, 1)], qT_hi[:, :], ALU.add,
                        ALU.subtract).then_inc(q_l, 1)
                if old:
                    dve.wait_ge(s_exp, done)
                    nc.vector.reciprocal(rden[:, :], den[:, :]).then_inc(s_rd, 1)
                    dve.wait_ge(s_rd, done)
                    dve.wait_ge(p_T, done - 1)
                    tt(pn[:, :, :], prob[:, :, :], rden[:, :].unsqueeze(2).broadcast_to([P, QUAD, T]),
                       ALU.mult).then_inc(s_pn, 1)
                if new:
                    dve.wait_ge(k_h, done + 1)
                    stt(kT_lo[:, :], bank[1][:, :], bT[:, cols(i + BQ + H, 1)], kT_hi[:, :], ALU.add,
                        ALU.subtract).then_inc(k_l, 1)
                if old:
                    dve.wait_ge(p_h, done)
                    tt(pT_lo[:, :], bank[4][:, :], pT_hi[:, :], ALU.subtract).then_inc(p_l, 1)
                if new:
                    dve.wait_ge(v_h, done + 1)
                    tt(v_lo[:, u, :], bank[2][:, :], v_hi[:, u, :], ALU.subtract).then_inc(v_l, 1)
                if old:
                    dve.wait_ge(a_h, done)
                    stt(aT_lo[:, :], bank[5][:, :], bT[:, cols(i + BQ + 2 * H - 1, 1)], aT_hi[:, :], ALU.add,
                        ALU.subtract).then_inc(a_l, 1)

            dve.wait_ge(ada_ok, 4)
            layer_norm(0, SH1, SC1)
            with dve.Fori(0, NG) as g:
                for i in range(4):
                    step(g, i, i % 2, True)
                with dve.Fori(4, H - 1, 2) as i:
                    for u in (0, 1):
                        step(g, i + u, u, False)
                step(g, H, 0, True)
                quad = cols(g * QUAD, QUAD)
                dve.wait_ge(o_gated, g + 1)
                for k in range(KD):
                    op = tt(xr2[:, k, quad, :], gated[:, k, :, :], xr[:, k, quad, :], ALU.add)
                op.then_inc(o_res, 1)
            layer_norm(1, SH2, SC2)
            with dve.Fori(0, NG) as g:
                for m in range(FM):
                    dve.wait_ge(f_hi, g * FM + (m + 1))
                    tt(hid_lo[:, m % 2, :], hf[:, m % 2, :], hid_hi[:, m % 2, :], ALU.subtract).then_inc(f_lo, 1)
                quad = cols(g * QUAD, QUAD)
                dve.wait_ge(f_gated, g + 1)
                dve.wait_ge(y_T, g * QUAD)
                for k in range(KD):
                    op = tt(yT[:, k, :, :], gated[:, k, :, :], xr2[:, k, quad, :], ALU.add)
                op.then_inc(f_sum, 1)
                dve.wait_ge(f_sum, g + 1)
                for k in range(KD):
                    op = tt(yT[:, k, :, :], yT[:, k, :, :], xr[:, k, quad, :], ALU.add)
                op.then_inc(f_out, 1)


_INS = ["x", "cond_2048", "L0_cond_W_ih", "L0_cond_W_hh", "L0_cond_b_ih", "L0_cond_b_hh", "L1_cond_ada_w",
        "L1_cond_ada_b", "L1_cond_qkv_w", "L1_cond_qkv_b", "L1_cond_out_w", "L1_cond_out_b", "L1_cond_ffn_w1",
        "L1_cond_ffn_b1", "L1_cond_ffn_w2", "L1_cond_ffn_b2"]


def kernel(**inputs):
    import numpy as _np
    import concourse.bacc as _bacc
    from concourse.bass_utils import run_bass_kernel_spmd as _run

    nc = _bacc.Bacc("TRN2", target_bir_lowering=False, num_devices=1)
    arrays, args = {}, []
    for name in _INS:
        a = _np.ascontiguousarray(inputs[name])
        arrays[f"in_{name}"] = a
        args.append(nc.dram_tensor(f"in_{name}", a.shape, mybir.dt.from_np(a.dtype), kind="ExternalInput").ap())
    args.append(nc.dram_tensor("out", (B, T, D), mybir.dt.float32, kind="ExternalOutput").ap())
    build(nc, *args)
    r = _run(nc, [arrays], core_ids=[0])
    return r.results[0]["out"]
```

```python
import concourse.bass as bass
from concourse import mybir
from contextlib import ExitStack
import math

P = 128
B, T, D = 16, 128, 256
KD = D // P
GATES = 3 * D
GM = GATES // P
H, DH = 16, 128
INNER = H * DH
MLP = 4 * D
FM = MLP // P
ADA = 6 * D // P
QUAD = 4
NG = B // QUAD
N = QUAD * T
BS = 8
NBL = T // BS
GB = KD * B
assert BS * B == P
EPS = 1e-6
SCALE = DH ** -0.5
CH = 1536
PIECE = CH // 3
WCOLS = (3 * INNER * KD + H * D + KD * MLP + FM * D)
NC = -(-WCOLS // CH)
assert NC == NBL - 2

LAG = 3
EARLY = 2

BI, BH, BA, BQ = 0, GM, 2 * GM, 2 * GM + ADA
BV = BQ + 2 * H
BO = BQ + 3 * H
B1 = BO + KD
B2 = B1 + FM
NB = B2 + KD
SH1, SC1, G1, SH2, SC2, G2 = (i * KD for i in range(6))


def build(nc, x, cond, W_ih, W_hh, b_ih, b_hh, ada_w, ada_b, qkv_w, qkv_b, out_w, out_b,
          f1_w, f1_b, f2_w, f2_b, out):
    f32, f16 = mybir.dt.float32, mybir.dt.float16
    ALU, ACT, AX = mybir.AluOpType, mybir.ActivationFunctionType, mybir.AxisListType
    ctx = ExitStack()
    with ctx:
        def sb(name, shape, dt=f32, scope=ctx):
            return scope.enter_context(nc.sbuf_tensor(name, shape, dt))

        def sem(name):
            return ctx.enter_context(nc.semaphore(name))

        ident = sb("ident", [P, P])
        ident16 = sb("ident16", [P, P], f16)
        w_hi = sb("w_hi", [P, NC * CH], f16)
        w_lo = sb("w_lo", [P, WCOLS], f16)
        bT = sb("bT", [P, NB])
        ada = sb("ada", [P, ADA, B])
        gbo = sb("gbo", [P, KD, B])
        gb2 = sb("gb2", [P, KD, B])
        xr = sb("xr", [P, KD, B, T])
        y_hi = sb("y_hi", [P, KD, B, T], f16)
        y_lo = sb("y_lo", [P, KD, B, T], f16)
        nhalf = sb("nhalf", [P, 8])
        gru = ExitStack()
        stage = sb("stage", [P, 2, CH], f32, gru)
        wg32 = sb("wg32", [P, 2, KD, GATES], f32, gru)
        adaw = sb("adaw", [P, KD, 6 * D], f32, gru)
        brow = sb("brow", [NB, P], f32, gru)
        crow = sb("crow", [B, D], f32, gru)
        whh_hi = sb("whh_hi", [P, KD, GATES], f16, gru)
        whh_lo = sb("whh_lo", [P, KD, GATES], f16, gru)
        wih_hi = sb("wih_hi", [P, KD, GATES], f16, gru)
        wih_lo = sb("wih_lo", [P, KD, GATES], f16, gru)
        bx32 = sb("bx32", [P, BS * GM * B], f32, gru)
        bx_hi = sb("bx_hi", [P, BS * GM * B], f16, gru)
        bx_lo = sb("bx_lo", [P, BS * GM * B], f16, gru)
        bx = sb("bx", [P, GM], f32, gru)
        bn32 = sb("bn32", [P, 2, BS, KD, B], f32, gru)
        condT = sb("condT", [P, KD, B], f32, gru)
        xin = sb("xin", [P, D], f32, gru)
        x32 = sb("x32", [P, 2, KD, P], f32, gru)
        xb_hi = sb("xb_hi", [P, KD, P], f16, gru)
        xb_lo = sb("xb_lo", [P, KD, P], f16, gru)
        grz = [sb(f"grz{i}", [P, 2, BS, 2 * GB], f16, gru) for i in (0, 1)]
        gnb = [sb(f"gnb{i}", [P, 2, BS, GB, 2], f16, gru) for i in (0, 1)]
        hs = sb("hs", [P, 2, BS, GB, 2], f32, gru)
        h_hi = sb("h_hi", [P, GB, 2], f16, gru)
        h_lo = sb("h_lo", [P, GB], f16, gru)
        zr = sb("zr", [P, GB, 2], f32, gru)
        zz = sb("zz", [P, GB, 2], f32, gru)
        nu = sb("nu", [P, GB, 2], f32, gru)
        zg = sb("zg", [P, GB], f32, gru)
        npre = sb("npre", [P, GB, 2], f32, gru)
        xrb = sb("xrb", [P, KD, P], f32, gru)
        natb = sb("natb", [P, D], f32, gru)
        stb = sb("stb", [P, 6], f32, gru)
        lb = sb("lb", [P, 8], f32, gru)
        xnb = sb("xnb", [P, D], f32, gru)
        ym = sb("ym", [P, KD, P], f32, gru)
        yb = sb("yb", [P, KD, P], f32, gru)
        gru.close()
        xr2 = sb("xr2", [P, KD, B, T])
        st6 = sb("st6", [P, QUAD, 6])
        part = sb("part", [P, 3, QUAD])
        mean = sb("mean", [P, QUAD])
        msq = sb("msq", [P, QUAD])
        mvar = sb("mvar", [P, QUAD])
        rstd = sb("rstd", [P, QUAD])
        veps = sb("veps", [P, QUAD])
        tin = sb("tin", [P, QUAD, KD, T])
        xn = sb("xn", [P, QUAD, D])
        yf = sb("yf", [P, QUAD, KD, T])
        qT_hi = sb("qT_hi", [P, N], f16)
        qT_lo = sb("qT_lo", [P, N], f16)
        kT_hi = sb("kT_hi", [P, N], f16)
        kT_lo = sb("kT_lo", [P, N], f16)
        v_hi = sb("v_hi", [P, 2, N], f16)
        v_lo = sb("v_lo", [P, 2, N], f16)
        pT_hi = sb("pT_hi", [P, N], f16)
        pT_lo = sb("pT_lo", [P, N], f16)
        aT_hi = sb("aT_hi", [P, N], f16)
        aT_lo = sb("aT_lo", [P, N], f16)
        prob = sb("prob", [P, QUAD, T])
        pn = sb("pn", [P, 2, QUAD, T])
        mx = sb("mx", [P, QUAD])
        nmx = sb("nmx", [P, QUAD])
        den = sb("den", [P, QUAD])
        rden = sb("rden", [P, QUAD])
        gated = sb("gated", [P, KD, QUAD, T])
        hf = sb("hf", [P, 2, N])
        hid_hi = sb("hid_hi", [P, 2, N], f16)
        hid_lo = sb("hid_lo", [P, 2, N], f16)
        yT = sb("yT", [P, KD, QUAD, T])
        ynat = sb("ynat", [P, B, D])

        bank = [ctx.enter_context(nc.psum_tensor(f"bank{i}", [P, 512], f32)) for i in range(8)]

        AT_O = KD * 3 * INNER
        AT_1 = AT_O + H * D
        AT_2 = AT_1 + KD * MLP
        wq_hi, wq_lo = (w[:, 0:AT_O].rearrange("p (k c) -> p k c", k=KD) for w in (w_hi, w_lo))
        wo_hi, wo_lo = (w[:, AT_O:AT_1] for w in (w_hi, w_lo))
        w1_hi, w1_lo = (w[:, AT_1:AT_2].rearrange("p (k c) -> p k c", k=KD) for w in (w_hi, w_lo))
        w2_hi, w2_lo = (w[:, AT_2:WCOLS].rearrange("p (m c) -> p m c", m=FM) for w in (w_hi, w_lo))

        def sems(names):
            return [sem(n) for n in names.split()]

        stage_in = sems("stage_in0 stage_in1")
        (rows_in, gatew_in, x_in, adaw_in, ident0, ident_ok, const_ok, small_T, small_sb, cond_ok, zeros_ok,
         wg_hi, wg_lo, ada_mm, ada_add, ada_ok, bx_a, bx_b, bx_c, bx_ok, bn_a, bn_ok, chunk_hi, chunk_lo) = sems(
             "rows_in gatew_in x_in adaw_in ident0 ident_ok const_ok small_T small_sb cond_ok zeros_ok "
             "wg_hi wg_lo ada_mm ada_add ada_ok bx_a bx_b bx_c bx_ok bn_a bn_ok chunk_hi chunk_lo")
        (r_mm, hn_mm, z_mm, r_ok, z_ok, oz_ok, n_ok, npre_ok, u_ok, hhi_ok, h32_ok, hlo_ok) = sems(
            "r_mm hn_mm z_mm r_ok z_ok oz_ok n_ok npre_ok u_ok hhi_ok h32_ok hlo_ok")
        xt_T, xt_32, xt_hi, xt_lo, rz_mm, nb_mm, rz_hi, nb_hi, rz_lo, nb_lo = sems(
            "xt_T xt_32 xt_hi xt_lo rz_mm nb_mm rz_hi nb_hi rz_lo nb_lo")
        xrb_ok, xr_ok, lb_T, lb_nat, lb_st, lb_a, lb_b, lb_c, lb_r, lb_xn, lb_B, lb_m, lb_y, lb_hi, lb_lo = sems(
            "xrb_ok xr_ok lb_T lb_nat lb_st lb_a lb_b lb_c lb_r lb_xn lb_B lb_m lb_y lb_hi lb_lo")
        (ln_in, ln_ag, ln_T, ln_st, ln_ve, ln_rstd, ln_xn, ln_B, ln_y, ln_hi, ln_lo) = sems(
            "ln_in ln_ag ln_T ln_st ln_ve ln_rstd ln_xn ln_B ln_y ln_hi ln_lo")
        (q_mm, k_mm, v_mm, s_mm, p_T, a_mm, o_mm, q_h, k_h, v_h, q_l, k_l, v_l, s_mx, s_nm, s_exp, s_rd, s_pn,
         p_h, p_l, a_h, a_l, o_gated, o_res) = sems(
             "q_mm k_mm v_mm s_mm p_T a_mm o_mm q_h k_h v_h q_l k_l v_l s_mx s_nm s_exp s_rd s_pn "
             "p_h p_l a_h a_l o_gated o_res")
        (f_up, f_gelu, f_hi, f_lo, f_down, rest_a, rest_ok, f_out, y_T, y_nat) = sems(
            "f_up f_gelu f_hi f_lo f_down rest_a rest_ok f_out y_T y_nat")
        y_out = sem("y_out")

        block = ctx.enter_context(nc.Block())

        qkv_v = qkv_w.rearrange("(k p) c -> p k c", p=P)
        wo_v = out_w.rearrange("(h p) d -> p h d", p=P)
        w1_v = f1_w.rearrange("(k p) c -> p k c", p=P)
        w2_v = f2_w.rearrange("(m p) d -> p m d", p=P)
        per_k, half, heads = 3 * INNER // CH, CH // 2, CH // D
        chunks = [[(half * i, qkv_v[:, c // per_k, (c % per_k) * CH + half * i:(c % per_k) * CH + half * (i + 1)])
                   for i in (0, 1)] for c in range(KD * per_k)]
        chunks += [[(half * i, wo_v[:, heads * c + heads // 2 * i:heads * c + heads // 2 * (i + 1), :]) for i in (0, 1)]
                   for c in (0, 1)]
        chunks += [[(0, wo_v[:, 2 * heads:H, :]), (2 * PIECE, w1_v[:, 0, 0:PIECE])],
                   [(0, w1_v[:, 0, PIECE:MLP]), (PIECE, w1_v[:, 1, :])],
                   [(0, w2_v[:, 0:3, :]), (half, w2_v[:, 3:6, :])],
                   [(0, w2_v[:, 6, :]), (D, w2_v[:, 7, :])]]
        assert len(chunks) == NC

        def cols(at, n):
            return slice(at, at + n) if isinstance(at, int) else bass.ds(at, n)

        @block.sync
        def _(sp):
            for at, src, n in ((BI, b_ih, GM), (BH, b_hh, GM), (BA, ada_b, ADA), (BQ, qkv_b, 3 * H), (BO, out_b, KD),
                               (B1, f1_b, FM), (B2, f2_b, KD)):
                sp.dma_start(brow[at:at + n, :], src.rearrange("(n p) -> n p", p=P)).then_inc(rows_in, 16)
            sp.dma_start(crow[:, :], cond).then_inc(rows_in, 16)
            for n, w in enumerate((W_ih, W_hh)):
                sp.dma_start(wg32[:, n, :, :], w.rearrange("(k p) c -> p k c", p=P)).then_inc(gatew_in, 16)
            def load_x(n):
                for t in range(BS):
                    sp.dma_start(xin[t * B:(t + 1) * B, :], x[:, n * BS + t, :]).then_inc(x_in, 16)

            def load_chunk(c):
                if c >= 2:
                    sp.wait_ge(chunk_lo, 3 * (c - 1))
                for at, src in chunks[c]:
                    n = math.prod(src.shape[1:])
                    dst = stage[:, c % 2, at:at + n]
                    sp.dma_start(dst if len(src.shape) == 2 else dst.rearrange("p (a b) -> p a b", a=src.shape[1]),
                                 src).then_inc(stage_in[c % 2], 16)

            load_x(0)
            sp.dma_start(adaw[:, :, :], ada_w.rearrange("(k p) c -> p k c", p=P)).then_inc(adaw_in, 16)
            for c in (0, 1):
                load_chunk(c)
            for n in range(1, NBL):
                sp.wait_ge(xt_T, n)
                load_x(n)
                if 3 <= n <= NC:
                    load_chunk(n - 1)
            out_v = out.rearrange("b t d -> t b d")
            with sp.Fori(0, NG - 1) as g:
                sp.wait_ge(y_nat, g * QUAD + QUAD)
                quad = cols(g * QUAD, QUAD)
                sp.dma_start(out_v[:, quad, :], ynat[:, quad, :]).then_inc(y_out, 16)
            for b in range(B - QUAD, B):
                sp.wait_ge(y_nat, b + 1)
                sp.dma_start(out_v[:, b, :], ynat[:, b, :]).then_inc(y_out, 16)
            sp.wait_ge(y_out, 16 * (NG - 1 + QUAD))

        @block.gpsimd
        def _(pool):
            nc.gpsimd.memset(ident[:, :], 0.0).then_inc(ident0, 1)
            pool.wait_ge(ident0, 1)
            nc.gpsimd.affine_select(out=ident[:, :], in_=ident[:, :], compare_op=ALU.not_equal, fill=1.0, base=0,
                                    pattern=[[-1, P]], channel_multiplier=1).then_inc(ident_ok, 1)
            pool.wait_ge(ident_ok, 1)
            nc.gpsimd.tensor_copy(ident16[:, :], ident[:, :]).then_inc(const_ok, 1)
            nc.gpsimd.memset(nhalf[:, :], -0.5).then_inc(const_ok, 1)
            mul, add, sub = ALU.mult, ALU.add, ALU.subtract
            gtt, gts = nc.gpsimd.tensor_tensor, nc.gpsimd.tensor_scalar

            def x_low(n):
                pool.wait_ge(xt_hi, n + 1)
                pool.wait_ge(xt_32, n + 1)
                gtt(xb_lo[:, :, :], x32[:, n % 2, :, :], xb_hi[:, :, :], sub).then_inc(xt_lo, 1)

            def keep_rows(n):
                pool.wait_ge(xrb_ok, KD * (n + 1))
                nc.gpsimd.tensor_copy(xr[:, :, :, cols(n * BS, BS)].rearrange("p k b t -> p k t b"),
                                      xrb[:, :, :].rearrange("p k (t b) -> p k t b", b=B)).then_inc(xr_ok, 1)

            def row_stats(n):
                even_mean, even_m2, odd_mean, odd_m2 = (stb[:, i:i + 1] for i in (1, 2, 4, 5))
                pool.wait_ge(lb_st, n + 1)
                gtt(lb[:, 0:1], even_mean, odd_mean, add)
                gtt(lb[:, 1:2], even_mean, odd_mean, sub)
                gtt(lb[:, 2:3], even_m2, odd_m2, add).then_inc(lb_a, 1)
                pool.wait_ge(lb_a, n + 1)
                gts(lb[:, 3:4], lb[:, 0:1], 0.5, None, mul)
                gtt(lb[:, 4:5], lb[:, 1:2], lb[:, 1:2], mul)
                gts(lb[:, 5:6], lb[:, 2:3], 1.0 / D, EPS, mul, add).then_inc(lb_b, 1)
                pool.wait_ge(lb_b, n + 1)
                gts(lb[:, 4:5], lb[:, 4:5], 0.25, None, mul).then_inc(lb_c, 1)
                pool.wait_ge(lb_c, 2 * n + 1)
                gtt(lb[:, 6:7], lb[:, 4:5], lb[:, 5:6], add).then_inc(lb_c, 1)
                pool.wait_ge(lb_c, 2 * n + 2)
                gtt(lb[:, 7:8], lb[:, 6:7], nhalf[:, 0:1], ALU.pow).then_inc(lb_r, 1)

            def y_low(n):
                pool.wait_ge(lb_hi, n + 1)
                at = cols(n * BS, BS)
                gtt(y_lo[:, :, :, at].rearrange("p k b t -> p k t b"),
                    yb[:, :, :].rearrange("p k (t b) -> p k t b", b=B),
                    y_hi[:, :, :, at].rearrange("p k b t -> p k t b"), sub).then_inc(lb_lo, 1)

            def split_chunk(c):
                for i in range(min(3, (WCOLS - c * CH) // PIECE)):
                    at = slice(c * CH + i * PIECE, c * CH + (i + 1) * PIECE)
                    pool.wait_ge(chunk_hi, 3 * c + i + 1)
                    gtt(w_lo[:, at], stage[:, c % 2, i * PIECE:(i + 1) * PIECE], w_hi[:, at], sub
                        ).then_inc(chunk_lo, 1)

            pool.wait_ge(const_ok, 2)
            x_low(0)
            for n in range(NBL + 1):
                if n < NBL - 1:
                    x_low(n + 1)
                if n > 0:
                    keep_rows(n - 1)
                    row_stats(n - 1)
                if 1 <= n <= NC:
                    split_chunk(n - 1)
                if n > 0:
                    y_low(n - 1)
            def norm_in(g):
                pool.wait_ge(o_res, g + 1)
                if not (isinstance(g, int) and g == 0):
                    pool.wait_ge(ln_T, g)
                nc.gpsimd.tensor_copy(tin[:, :, :, :].rearrange("p j k t -> p k j t"),
                                      xr2[:, :, cols(g * QUAD, QUAD), :]).then_inc(ln_in, 1)

            def norm_rstd(g):
                pool.wait_ge(ln_ve, g + 1)
                gtt(rstd[:, :], veps[:, :], nhalf[:, 0:QUAD], ALU.pow).then_inc(ln_rstd, 1)

            def norm_low(g):
                pool.wait_ge(ln_hi, g + 1)
                quad = cols(g * QUAD, QUAD)
                gtt(y_lo[:, :, quad, :].rearrange("p k j t -> p j k t"), yf[:, :, :, :],
                    y_hi[:, :, quad, :].rearrange("p k j t -> p j k t"), sub).then_inc(ln_lo, 1)

            def sum_rest(g):
                quad = cols(g * QUAD, QUAD)
                pool.wait_ge(o_res, g + 1)
                for k in range(KD):
                    gtt(xr[:, k, quad, :], xr[:, k, quad, :],
                        gb2[:, k, quad].unsqueeze(2).broadcast_to([P, QUAD, T]), add).then_inc(rest_a, 1)
                pool.wait_ge(rest_a, g * KD + KD)
                gtt(xr[:, :, quad, :], xr[:, :, quad, :], xr2[:, :, quad, :], add).then_inc(rest_ok, 1)

            norm_in(0)
            with pool.Fori(0, NG - 1) as g:
                sum_rest(g)
            with pool.Fori(0, NG - 1) as g:
                norm_rstd(g)
                norm_in(g + 1)
                norm_low(g)
            norm_rstd(NG - 1)
            norm_low(NG - 1)
            sum_rest(NG - 1)

        @block.tensor
        def _(pe):
            def product(ps, w, a, start, stop):
                mm = nc.tensor.matmul
                mm(ps, w[0], a[0], start=start, stop=False, skip_group_check=True)
                mm(ps, w[1], a[0], start=False, stop=False, skip_group_check=True)
                return mm(ps, w[0], a[1], start=False, stop=stop, skip_group_check=True)

            def x_block_T(n):
                pe.wait_ge(x_in, (n + 1) * (16 * BS))
                if not (isinstance(n, int) and n == 0):
                    pe.wait_ge(xt_hi, n)
                    pe.wait_ge(xt_32, n)
                for k in range(KD):
                    mm = nc.tensor.transpose(bank[1][:, k * P:(k + 1) * P], xin[:, k * P:(k + 1) * P], ident[:, :])
                mm.then_inc(xt_T, 1)

            def x_bias(n, rz):
                cut = BS * 2 * GB
                ps, at, last_read = (bank[2], slice(0, cut), rz_lo) if rz else (bank[3], slice(cut, None), nb_lo)
                if not (isinstance(n, int) and n == 0):
                    pe.wait_ge(last_read, 2 * n if rz else n)
                for half, first in ((bx_hi, True), (bx_lo, False)):
                    nc.tensor.matmul(ps[:, 0:cut if rz else cut // 2], ident16[:, :], half[:, at], start=first,
                                     stop=False, skip_group_check=True)

            def x_tile(n, m):
                if m == 4:
                    pe.wait_ge(xt_lo, n + 1)
                ps, i, width = (bank[2], m, 4 * B) if m < 4 else (bank[3], m - 4, 2 * B)
                ps = ps[:, 0:BS * width].rearrange("p (t c) -> p t c", c=width)[:, :, i * B:(i + 1) * B]
                w = slice(m * P, (m + 1) * P)
                for k in range(KD):
                    mm = product(ps, (wih_hi[:, k, w], wih_lo[:, k, w]), (xb_hi[:, k, :], xb_lo[:, k, :]), False,
                                 k == KD - 1)
                if m in (3, 5):
                    mm.then_inc(nb_mm if m == 5 else rz_mm, 1)

            def rows_T(n):
                pe.wait_ge(xrb_ok, (n + 1) * KD)
                for k in range(KD):
                    mm = nc.tensor.transpose(bank[4][:, k * P:(k + 1) * P], xrb[:, k, :], ident[:, :])
                mm.then_inc(lb_T, 1)

            def rows_back(n):
                pe.wait_ge(lb_xn, n + 1)
                for k in range(KD):
                    mm = nc.tensor.transpose(bank[5][:, k * P:(k + 1) * P], xnb[:, k * P:(k + 1) * P], ident[:, :])
                mm.then_inc(lb_B, 1)

            pe.wait_ge(ident_ok, 1)
            pe.wait_ge(rows_in, 16 * 8)
            nc.tensor.transpose(bank[0][:, 0:NB], brow[:, :], ident[0:NB, 0:NB])
            for k in range(KD):
                mm = nc.tensor.transpose(bank[0][:, P + k * B:P + (k + 1) * B], crow[:, k * P:(k + 1) * P],
                                         ident[0:B, 0:B])
            mm.then_inc(small_T, 1)
            x_block_T(0)
            pe.wait_ge(bx_ok, 1)
            pe.wait_ge(const_ok, 1)
            pe.wait_ge(wg_lo, 1)
            x_bias(0, False)
            for m in (4, 5):
                x_tile(0, m)
            x_bias(0, True)
            for m in range(4):
                x_tile(0, m)
            pe.wait_ge(wg_lo, 2)

            def modulation(tiles):
                for m in tiles:
                    for k in range(KD):
                        mm = nc.tensor.matmul(bank[5][:, m * B:(m + 1) * B], adaw[:, k, m * P:(m + 1) * P],
                                              condT[:, k, :], start=(k == 0), stop=(k == KD - 1))
                if tiles[-1] == ADA - 1:
                    mm.then_inc(ada_mm, 1)

            pe.wait_ge(bn_ok, 2)
            rb, hb, zb = bank[0], bank[6], bank[7]
            hb2 = hb[:, 0:2 * GB].rearrange("p (j s) -> p j s", s=2)

            def gru_step(r, par, s):
                t1 = r * BS + (s + 1)
                if s == 0:
                    pe.wait_ge(rz_lo, r * 2 + 1)
                    pe.wait_ge(nb_lo, r + 1)
                if s == BS // 2:
                    pe.wait_ge(rz_lo, r * 2 + 2)
                pe.wait_ge(oz_ok, t1)
                for ps, c in ((rb, 0), (zb, GB)):
                    for i in (0, 1):
                        nc.tensor.matmul(ps[:, 0:GB], ident16[:, :], grz[i][:, par, s, c:c + GB], start=(i == 0),
                                         stop=False, skip_group_check=True)
                pe.wait_ge(npre_ok, t1)
                for i in (0, 1):
                    nc.tensor.matmul(hb[:, 0:2 * GB], ident16[:, :], gnb[i][:, par, s, :, :], start=(i == 0),
                                     stop=False, skip_group_check=True)
                pe.wait_ge(hhi_ok, t1)
                r_sums = (0, lambda m: rb[:, m * B:(m + 1) * B])
                hn_sums = (4, lambda m: hb2[:, m * B:(m + 1) * B, 0])
                z_sums = (2, lambda m: zb[:, m * B:(m + 1) * B])

                def gate(sums, high):
                    m0, out = sums
                    for m in range(2):
                        for k in range(KD):
                            w = slice((m0 + m) * P, (m0 + m + 1) * P)
                            a = h_hi[:, k * B:(k + 1) * B, 1] if high else h_lo[:, k * B:(k + 1) * B]
                            for half in (whh_hi, whh_lo) if high else (whh_hi,):
                                mm = nc.tensor.matmul(out(m), half[:, k, w], a, start=False, stop=not high,
                                                      skip_group_check=True)
                    return mm

                gate(r_sums, True)
                gate(hn_sums, True)
                pe.wait_ge(hlo_ok, t1)
                gate(r_sums, False).then_inc(r_mm, 1)
                gate(hn_sums, False).then_inc(hn_mm, 1)
                gate(z_sums, True)
                gate(z_sums, False).then_inc(z_mm, 1)

            def gru_block(r, par, rows, ahead):
                for s in range(BS):
                    gru_step(r, par, s)
                    if ahead:
                        if s == 0:
                            x_block_T(r + 1)
                            x_bias(r + 1, False)
                        elif s == 1:
                            x_bias(r + 1, True)
                        for m in tiles.get(s, ()):
                            x_tile(r + 1, m)
                    if rows and s == 2:
                        rows_T(r - 1)
                    if rows and s == 5:
                        rows_back(r - 1)
                    if not rows and s < 7:
                        pe.wait_ge(adaw_in, 16)
                        modulation({0: (0, 1), 1: (2, 3), 2: (4, 5), 3: (6,), 4: (7,), 5: (8,), 6: (9, 10, 11)}[s])

            tiles = {2: (4,), 3: (5, 0), 4: (1, 2), 5: (3,)}
            gru_block(0, 0, False, True)
            with pe.Fori(1, NBL - 2, 2) as r:
                gru_block(r, 1, True, True)
                gru_block(r + 1, 0, True, True)
            gru_block(NBL - 1, 1, True, False)
            rows_T(NBL - 1)
            rows_back(NBL - 1)
            pe.wait_ge(lb_lo, NBL)
            pe.wait_ge(chunk_lo, WCOLS // PIECE)

            def norm_rows(g, base=6):
                pe.wait_ge(ln_in, g + 1)
                if not (isinstance(g, int) and g == 0):
                    pe.wait_ge(ln_y, g)
                for i in range(QUAD * KD):
                    j, k = i // KD, i % KD
                    at = (j % 2 * KD + k) * P
                    mm = nc.tensor.transpose(bank[base + j // 2][:, at:at + P], tin[:, j, k, :], ident[:, :])
                mm.then_inc(ln_T, 1)

            def norm_back(g, base=6):
                pe.wait_ge(ln_xn, g + 1)
                for i in range(QUAD * KD):
                    j, k = i // KD, i % KD
                    at = (j % 2 * KD + k) * P
                    mm = nc.tensor.transpose(bank[base + j // 2][:, at:at + P], xn[:, j, k * P:(k + 1) * P], ident[:, :])
                mm.then_inc(ln_B, 1)

            def project_out(g, head, first, last):
                pe.wait_ge(a_l, g * H + (head + 1))
                for k in range(KD):
                    w = cols(head * D + k * P, P)
                    mm = product(bank[6 + k][:, :], (wo_hi[:, w], wo_lo[:, w]), (aT_hi[:, :], aT_lo[:, :]),
                                 first, last)
                if last:
                    mm.then_inc(o_mm, 1)

            def step(g, i, u, new=True, old=True, add=None):
                done = g * H + i
                some = not (isinstance(done, int) and done == 0)
                quad = cols(g * QUAD, QUAD)
                y = [(y_hi[:, k, quad, :], y_lo[:, k, quad, :]) for k in range(KD)]
                if old:
                    pe.wait_ge(s_pn, done - 1)
                    for j in range(QUAD):
                        mm = nc.tensor.transpose(bank[4][:, j * T:(j + 1) * T], pn[:, u, j, :], ident[:, :])
                    mm.then_inc(p_T, 1)
                if new:
                    if some:
                        pe.wait_ge(q_l, done)
                    for k in range(KD):
                        w = cols(i * DH, DH)
                        mm = product(bank[0][:, :], (wq_hi[:, k, w], wq_lo[:, k, w]), y[k], k == 0, k == KD - 1)
                    mm.then_inc(q_mm, 1)
                if add:
                    project_out(*add)
                if new:
                    if some:
                        pe.wait_ge(k_l, done)
                    for k in range(KD):
                        w = cols((i + H) * DH, DH)
                        mm = product(bank[1][:, :], (wq_hi[:, k, w], wq_lo[:, k, w]), y[k], k == 0, k == KD - 1)
                    mm.then_inc(k_mm, 1)
                if old:
                    pe.wait_ge(p_l, done - 1)
                    for j in range(QUAD):
                        c = slice(j * T, (j + 1) * T)
                        mm = product(bank[5][:, c], (v_hi[:, u, c], v_lo[:, u, c]), (pT_hi[:, c], pT_lo[:, c]),
                                     j == 0, True)
                    mm.then_inc(a_mm, 1)
                if new:
                    if some:
                        pe.wait_ge(v_l, done)
                    w = cols((i + 2 * H) * DH, DH)
                    for j in range(QUAD):
                        for k in range(KD):
                            mm = product(bank[2][:, j * DH:(j + 1) * DH],
                                         (y_hi[:, k, g * QUAD + j, :], y_lo[:, k, g * QUAD + j, :]),
                                         (wq_hi[:, k, w], wq_lo[:, k, w]), j == 0 and k == 0, k == KD - 1)
                    mm.then_inc(v_mm, 1)
                    pe.wait_ge(q_l, done + 1)
                    pe.wait_ge(k_l, done + 1)
                    if some:
                        pe.wait_ge(s_exp, done)
                    for j in range(QUAD):
                        c = slice(j * T, (j + 1) * T)
                        mm = product(bank[3][:, c], (qT_hi[:, c], qT_lo[:, c]), (kT_hi[:, c], kT_lo[:, c]),
                                     j == 0, True)
                    mm.then_inc(s_mm, 1)

            def middle(g):
                step(g, LAG, LAG % 2, add=(g, 0, True, False))
                with pe.Fori(LAG + 1, H - 1, 2) as i:
                    for u in (0, 1):
                        step(g, i + u, u, add=(g, i + (u - LAG), False, False))

            for i in range(LAG):
                step(0, i, i % 2, old=i >= 2)
            with pe.Fori(0, NG - 1) as g:
                middle(g)
                for i in range(LAG):
                    step(g + 1, i, i % 2, add=(g, H - LAG + i, False, i == LAG - 1))
                pe.wait_ge(o_gated, g + 1)
            middle(NG - 1)
            norm_rows(0, 0)
            for i in range(LAG):
                step(NG - 1, H + i, i % 2, new=False, old=i < 2, add=(NG - 1, H - LAG + i, False, i == LAG - 1))
            norm_back(0, 0)

            def up(g, m):
                first = isinstance(g, int) and g == 0
                quad = cols(g * QUAD, QUAD)
                if m == 0:
                    pe.wait_ge(ln_lo, g + 1)
                if not (first and m < 2):
                    pe.wait_ge(f_gelu, g * FM + (m - 1))
                w = slice(m * P, (m + 1) * P)
                for k in range(KD):
                    mm = product(bank[m % 2][:, :], (w1_hi[:, k, w], w1_lo[:, k, w]),
                                 (y_hi[:, k, quad, :], y_lo[:, k, quad, :]), k == 0, k == KD - 1)
                mm.then_inc(f_up, 1)

            def down(g, m):
                pe.wait_ge(f_lo, g * FM + (m + 1))
                if m == 0 and not (isinstance(g, int) and g == 0):
                    pe.wait_ge(f_out, g * QUAD)
                for k in range(KD):
                    w, a = slice(k * P, (k + 1) * P), m % 2
                    mm = product(bank[4 + k][:, :], (w2_hi[:, m, w], w2_lo[:, m, w]),
                                 (hid_hi[:, a, :], hid_lo[:, a, :]), m == 0, m == FM - 1)
                mm.then_inc(f_down, 1)

            def rows_out(g):
                for j in range(QUAD):
                    pe.wait_ge(f_out, g * QUAD + (j + 1))
                    if j >= 2:
                        pe.wait_ge(y_nat, g * QUAD + (j - 1))
                    for k in range(KD):
                        mm = nc.tensor.transpose(bank[2 + j % 2][:, k * P:(k + 1) * P], yT[:, k, j, :], ident[:, :])
                    mm.then_inc(y_T, 1)

            def tiles_to_end(g, normalise):
                for m in range(EARLY, FM):
                    up(g, m)
                    down(g, m - 1)
                    if normalise and m == EARLY:
                        norm_rows(g + 1)
                    if normalise and m == EARLY + 3:
                        norm_back(g + 1)

            up(0, 0)
            up(0, 1)
            down(0, 0)
            with pe.Fori(0, NG - 1) as g:
                tiles_to_end(g, True)
                up(g + 1, 0)
                down(g, FM - 1)
                up(g + 1, 1)
                rows_out(g)
                down(g + 1, 0)
            tiles_to_end(NG - 1, False)
            down(NG - 1, FM - 1)
            rows_out(NG - 1)

        @block.scalar
        def _(act):
            copy, ident_f = ACT.Copy, ACT.Identity
            def x_full(n, par):
                act.wait_ge(xt_T, n + 1)
                if not (isinstance(n, int) and n < 2):
                    act.wait_ge(xrb_ok, (n - 1) * KD)
                nc.scalar.activation(x32[:, par, :, :], bank[1][:, 0:D].rearrange("p (k c) -> p k c", k=KD),
                                     copy).then_inc(xt_32, 1)

            def x_high(n):
                act.wait_ge(xt_T, n + 1)
                nc.scalar.activation(xb_hi[:, :, :], bank[1][:, 0:D].rearrange("p (k c) -> p k c", k=KD),
                                     copy).then_inc(xt_hi, 1)

            def rz_high(n, par):
                act.wait_ge(rz_mm, n + 1)
                nc.scalar.activation(grz[0][:, par, :, :], bank[2][:, :].rearrange("p (t c) -> p t c", t=BS), copy
                                     ).then_inc(rz_hi, 1)

            def nb_high(n, par):
                act.wait_ge(nb_mm, n + 1)
                nc.scalar.activation(gnb[0][:, par, :, :, 1], bank[3][:, 0:BS * GB].rearrange("p (t c) -> p t c", t=BS),
                                     copy).then_inc(nb_hi, 1)

            def rows_full(n):
                act.wait_ge(lb_T, n + 1)
                nc.scalar.activation(natb[:, :], bank[4][:, 0:D], copy).then_inc(lb_nat, 1)

            def y_high(n):
                act.wait_ge(lb_y, n + 1)
                for k in range(KD):
                    op = nc.scalar.activation(y_hi[:, k, :, cols(n * BS, BS)].rearrange("p b t -> p t b"),
                                              yb[:, k, :].rearrange("p (t b) -> p t b", b=B), copy)
                op.then_inc(lb_hi, 1)

            def piece_high(r, par, i):
                if i == 0:
                    act.wait_ge(stage_in[1 - par], (r + par) * 16)
                nc.scalar.activation(w_hi[:, cols((r - 1) * CH + i * PIECE, PIECE)],
                                     stage[:, 1 - par, i * PIECE:(i + 1) * PIECE], copy).then_inc(chunk_hi, 1)

            act.wait_ge(npre_ok, 1)
            nc.scalar.activation(zg[:, :], zr[:, :, 0], ACT.Sigmoid).then_inc(oz_ok, 1)
            act.wait_ge(gatew_in, 32)
            nc.scalar.activation(wih_hi[:, :, :], wg32[:, 0, :, :], copy).then_inc(wg_hi, 1)
            x_high(0)
            x_full(0, 0)
            nc.scalar.activation(whh_hi[:, :, :], wg32[:, 1, :, :], copy).then_inc(wg_hi, 1)
            act.wait_ge(bn_ok, 1)
            nb_high(0, 0)
            rz_high(0, 0)

            def gru_block(r, par, rows, ahead):
                for s in range(BS):
                    t1 = r * BS + (s + 1)
                    act.wait_ge(r_mm, t1)
                    nc.scalar.activation(zr[:, :, 1], bank[0][:, 0:GB], ACT.Sigmoid).then_inc(r_ok, 1)
                    act.wait_ge(z_mm, t1)
                    nc.scalar.activation(zg[:, :], bank[7][:, 0:GB], ACT.Sigmoid).then_inc(z_ok, 1)
                    nc.scalar.activation(zz[:, :, 1], bank[7][:, 0:GB], ACT.Sigmoid, scale=-1.0).then_inc(oz_ok, 1)
                    act.wait_ge(npre_ok, t1 + 1)
                    nc.scalar.activation(nu[:, :, 0], npre[:, :, 1], ACT.Tanh).then_inc(n_ok, 1)
                    if ahead:
                        if s == 0:
                            x_high(r + 1)
                        elif s == 1:
                            x_full(r + 1, 1 - par)
                        elif s == 4:
                            nb_high(r + 1, 1 - par)
                        elif s == 5:
                            rz_high(r + 1, 1 - par)
                    if rows and s == 2:
                        rows_full(r - 1)
                    if rows and ahead and s in (3, 4, 6):
                        piece_high(r, par, {3: 0, 4: 1, 6: 2}[s])
                    if rows and s == 7:
                        y_high(r - 1)

            gru_block(0, 0, False, True)
            with act.Fori(1, NBL - 2, 2) as r:
                gru_block(r, 1, True, True)
                gru_block(r + 1, 0, True, True)
            gru_block(NBL - 1, 1, True, False)
            rows_full(NBL - 1)
            y_high(NBL - 1)

            def norm_high(g):
                act.wait_ge(ln_y, g + 1)
                nc.scalar.activation(y_hi[:, :, cols(g * QUAD, QUAD), :].rearrange("p k j t -> p j k t"),
                                     yf[:, :, :, :], copy).then_inc(ln_hi, 1)

            def gate_out(g):
                act.wait_ge(o_mm, g + 1)
                for k in range(KD):
                    for j in range(QUAD):
                        b = g * QUAD + j
                        op = nc.scalar.activation(gated[:, k, j, :], bank[6 + k][:, j * T:(j + 1) * T], ident_f,
                                                  bias=gbo[:, k, cols(b, 1)], scale=ada[:, G1 + k, cols(b, 1)])
                op.then_inc(o_gated, 1)

            def step(g, i, u, new=True, soft=True, old=None, gated_group=None):
                done = g * H + i
                if old is not None:
                    act.wait_ge(p_T, done - 1)
                    nc.scalar.activation(pT_hi[:, :], bank[4][:, :], copy).then_inc(p_h, 1)
                if soft:
                    act.wait_ge(s_nm, done)
                    if not (isinstance(done, int) and done == 1):
                        act.wait_ge(s_pn, done - 1)
                    for j in range(QUAD):
                        op = nc.scalar.activation(prob[:, j, :], bank[3][:, j * T:(j + 1) * T], ACT.Exp,
                                                  bias=nmx[:, j:j + 1], scale=SCALE, accum_out=den[:, j:j + 1])
                    op.then_inc(s_exp, 1)
                if new:
                    act.wait_ge(q_mm, done + 1)
                    if soft:
                        act.wait_ge(s_mm, done)
                    nc.scalar.activation(qT_hi[:, :], bank[0][:, :], ident_f,
                                         bias=bT[:, cols(i + BQ, 1)]).then_inc(q_h, 1)
                    act.wait_ge(k_mm, done + 1)
                    nc.scalar.activation(kT_hi[:, :], bank[1][:, :], ident_f,
                                         bias=bT[:, cols(i + BQ + H, 1)]).then_inc(k_h, 1)
                if gated_group is not None:
                    gate_out(gated_group)
                if old is not None:
                    act.wait_ge(a_mm, done - 1)
                    nc.scalar.activation(aT_hi[:, :], bank[5][:, :], ident_f,
                                         bias=bT[:, cols(old, 1)]).then_inc(a_h, 1)
                if new:
                    act.wait_ge(v_mm, done + 1)
                    nc.scalar.activation(v_hi[:, u, :], bank[2][:, :], copy).then_inc(v_h, 1)

            def middle(g):
                step(g, LAG, LAG % 2, old=BV + LAG - 2)
                with act.Fori(LAG + 1, H - 1, 2) as i:
                    for u in (0, 1):
                        step(g, i + u, u, old=i + (BV + u - 2))

            for i in range(LAG):
                step(0, i, i % 2, soft=i >= 1, old=BV + i - 2 if i >= 2 else None)
            with act.Fori(0, NG - 1) as g:
                middle(g)
                for i in range(LAG):
                    step(g + 1, i, i % 2, old=BV + (i - 2) % H, gated_group=g if i == LAG - 1 else None)
            middle(NG - 1)
            for i in (0, 1):
                step(NG - 1, H + i, i % 2, new=False, soft=i == 0, old=BV + H + i - 2)
            norm_high(0)
            gate_out(NG - 1)

            def feed_forward(g, m):
                first = isinstance(g, int) and g == 0
                act.wait_ge(f_up, g * FM + (m + 1))
                if not (first and m < 2):
                    act.wait_ge(f_lo, g * FM + (m - 1))
                nc.scalar.activation(hf[:, m % 2, :], bank[m % 2][:, :], ACT.Gelu,
                                     bias=bT[:, B1 + m:B1 + m + 1]).then_inc(f_gelu, 1)
                act.wait_ge(f_gelu, g * FM + (m + 1))
                if not (first and m < 2):
                    act.wait_ge(f_down, g * FM + (m - 1))
                nc.scalar.activation(hid_hi[:, m % 2, :], hf[:, m % 2, :], copy).then_inc(f_hi, 1)

            def rows_out(g):
                for j in range(QUAD):
                    act.wait_ge(y_T, g * QUAD + (j + 1))
                    nc.scalar.activation(ynat[:, cols(g * QUAD + j, 1), :],
                                         bank[2 + j % 2][:, 0:D].unsqueeze(1), copy).then_inc(y_nat, 1)

            for m in range(EARLY):
                feed_forward(0, m)
            with act.Fori(0, NG - 1) as g:
                for m in range(EARLY, FM):
                    feed_forward(g, m)
                    if m == EARLY + 4:
                        norm_high(g + 1)
                for m in range(EARLY):
                    feed_forward(g + 1, m)
                rows_out(g)
            for m in range(EARLY, FM):
                feed_forward(NG - 1, m)
            rows_out(NG - 1)

        @block.vector
        def _(dve):
            tt, ts, stt = nc.vector.tensor_tensor, nc.vector.tensor_scalar, nc.vector.scalar_tensor_tensor
            copy = nc.vector.tensor_copy
            nc.vector.memset(zr[:, :, :], 0.0)
            nc.vector.memset(zz[:, :, :], 0.0)
            nc.vector.memset(npre[:, :, :], 0.0).then_inc(npre_ok, 1)
            dve.wait_ge(npre_ok, 1)
            dve.wait_ge(small_T, 1)
            copy(bT[:, :], bank[0][:, 0:NB]).then_inc(small_sb, 1)
            copy(condT[:, :, :], bank[0][:, P:P + GB].rearrange("p (k b) -> p k b", k=KD)).then_inc(cond_ok, 1)
            dve.wait_ge(small_sb, 1)
            tt(bx[:, 0:4], bT[:, BI:BI + 4], bT[:, BH:BH + 4], ALU.add).then_inc(bx_a, 1)
            copy(bx[:, 4:6], bT[:, BI + 4:BI + 6]).then_inc(bx_a, 1)
            copy(bn32[:, :, :, :, :].rearrange("p r t k b -> p (r t) k b"),
                 bT[:, BH + 4:BH + 6].unsqueeze(1).unsqueeze(3).broadcast_to([P, 2 * BS, KD, B])).then_inc(bn_a, 1)
            dve.wait_ge(bx_a, 2)
            rz = BS * 2 * GB
            for at, n_tiles, m0 in ((0, 4, 0), (rz, 2, 4)):
                copy(bx32[:, at:at + BS * n_tiles * B].rearrange("p (t m b) -> p t m b", t=BS, m=n_tiles),
                     bx[:, m0:m0 + n_tiles].unsqueeze(1).unsqueeze(3).broadcast_to([P, BS, n_tiles, B])
                     ).then_inc(bx_b, 1)
            dve.wait_ge(bn_a, 1)
            bn = bn32[:, :, :, :, :].rearrange("p r t k b -> p (r t k b)")
            nb = [g[:, :, :, :, 0].rearrange("p r t j -> p (r t j)") for g in gnb]
            copy(nb[0], bn).then_inc(bn_ok, 1)
            dve.wait_ge(bx_b, 2)
            copy(bx_hi[:, :], bx32[:, :]).then_inc(bx_c, 1)
            dve.wait_ge(bn_ok, 1)
            tt(nb[1], bn, nb[0], ALU.subtract).then_inc(bn_ok, 1)
            dve.wait_ge(bx_c, 1)
            tt(bx_lo[:, :], bx32[:, :], bx_hi[:, :], ALU.subtract).then_inc(bx_ok, 1)
            dve.wait_ge(cond_ok, 1)
            cond_row = condT[:, :, :].rearrange("p k b -> p (k b)")
            copy(hs[:, 1, BS - 1, :, 1], cond_row).then_inc(zeros_ok, 1)
            copy(h_hi[:, :, 1], cond_row).then_inc(hhi_ok, 1)
            dve.wait_ge(hhi_ok, 1)
            tt(h_lo[:, :], cond_row, h_hi[:, :, 1], ALU.subtract).then_inc(hlo_ok, 1)
            for n, (hi, lo) in enumerate(((wih_hi, wih_lo), (whh_hi, whh_lo))):
                dve.wait_ge(wg_hi, n + 1)
                tt(lo[:, :, :], wg32[:, n, :, :], hi[:, :, :], ALU.subtract).then_inc(wg_lo, 1)
            def modulation():
                dve.wait_ge(ada_mm, 1)
                tt(ada[:, :, :], bank[5][:, 0:ADA * B].rearrange("p (m b) -> p m b", b=B),
                   bT[:, BA:BA + ADA].unsqueeze(2).broadcast_to([P, ADA, B]), ALU.add).then_inc(ada_add, 1)
                dve.wait_ge(ada_add, 1)
                for sc in (SC1, SC2):
                    nc.vector.tensor_scalar_add(ada[:, sc:sc + KD, :], ada[:, sc:sc + KD, :], 1.0).then_inc(ada_ok, 1)
                for dst, gate_tile, bias in ((gbo, G1, BO), (gb2, G2, B2)):
                    tt(dst[:, :, :], ada[:, gate_tile:gate_tile + KD, :],
                       bT[:, bias:bias + KD].unsqueeze(2).broadcast_to([P, KD, B]), ALU.mult).then_inc(ada_ok, 1)

            def rz_low(n, par, half):
                t, c = slice(half * BS // 2, (half + 1) * BS // 2), BS * GB
                if half == 0:
                    dve.wait_ge(rz_hi, n + 1)
                tt(grz[1][:, par, t, :], bank[2][:, half * c:(half + 1) * c].rearrange("p (t c) -> p t c", t=BS // 2),
                   grz[0][:, par, t, :], ALU.subtract).then_inc(rz_lo, 1)

            def nb_low(n, par):
                dve.wait_ge(nb_hi, n + 1)
                tt(gnb[1][:, par, :, :, 1], bank[3][:, 0:BS * GB].rearrange("p (t c) -> p t c", t=BS),
                   gnb[0][:, par, :, :, 1], ALU.subtract).then_inc(nb_lo, 1)

            def rows_sum(n, par, k):
                if k == 0:
                    dve.wait_ge(h32_ok, (n + 1) * BS)
                    if not (isinstance(n, int) and n == 0):
                        dve.wait_ge(xr_ok, n)
                tt(xrb[:, k, :].rearrange("p (t b) -> p t b", b=B),
                   x32[:, par, k, :].rearrange("p (t b) -> p t b", b=B),
                   hs[:, par, :, k * B:(k + 1) * B, 1], ALU.add).then_inc(xrb_ok, 1)

            def rows_stats(n):
                dve.wait_ge(lb_nat, n + 1)
                nc.vector.bn_stats(stb[:, :], natb[:, :]).then_inc(lb_st, 1)

            def rows_norm(n):
                dve.wait_ge(lb_r, n + 1)
                ts(xnb[:, :], natb[:, :], lb[:, 3:4], lb[:, 7:8], ALU.subtract, ALU.mult).then_inc(lb_xn, 1)

            def modulate(dst, src, tile, op, done, n):
                tt(dst[:, :, :].rearrange("p k (t b) -> p k t b", b=B), src.rearrange("p (k t b) -> p k t b", k=KD, b=B),
                   ada[:, tile:tile + KD, :].unsqueeze(2).broadcast_to([P, KD, BS, B]), op).then_inc(done, 1)

            def rows_scale(n):
                dve.wait_ge(lb_B, n + 1)
                dve.wait_ge(ada_ok, 4)
                modulate(ym, bank[5][:, 0:D], SC1, ALU.mult, lb_m, n)

            def rows_shift(n):
                dve.wait_ge(lb_m, n + 1)
                if not (isinstance(n, int) and n == 0):
                    dve.wait_ge(lb_lo, n)
                modulate(yb, ym[:, :, :].rearrange("p k c -> p (k c)"), SH1, ALU.add, lb_y, n)

            nb_low(0, 0)
            for half in (0, 1):
                rz_low(0, 0, half)

            def gru_block(r, par, rows, ahead):
                for s in range(BS):
                    t1 = r * BS + (s + 1)
                    dve.wait_ge(r_ok, t1)
                    dve.wait_ge(hn_mm, t1)
                    nc.vector.tensor_tensor_scan(npre[:, :, :].rearrange("p j s -> p (j s)"),
                                                 zr[:, :, :].rearrange("p j s -> p (j s)"), bank[6][:, 0:2 * GB], 0.0,
                                                 ALU.mult, ALU.add).then_inc(npre_ok, 1)
                    dve.wait_ge(z_ok, t1)
                    before = hs[:, 1 - par, BS - 1, :, 1] if s == 0 else hs[:, par, s - 1, :, 1]
                    tt(nu[:, :, 1], zg[:, :], before, ALU.mult).then_inc(u_ok, 1)
                    dve.wait_ge(u_ok, t1)
                    dve.wait_ge(n_ok, t1)
                    gates = (zz[:, :, :].rearrange("p j s -> p (j s)"), nu[:, :, :].rearrange("p j s -> p (j s)"),
                             0.0, ALU.mult, ALU.add)
                    nc.vector.tensor_tensor_scan(h_hi[:, :, :].rearrange("p j s -> p (j s)"), *gates
                                                 ).then_inc(hhi_ok, 1)
                    nc.vector.tensor_tensor_scan(hs[:, par, s, :, :].rearrange("p j s -> p (j s)"), *gates
                                                 ).then_inc(h32_ok, 1)
                    dve.wait_ge(h32_ok, t1)
                    tt(h_lo[:, :], hs[:, par, s, :, 1], h_hi[:, :, 1], ALU.subtract).then_inc(hlo_ok, 1)
                    if s == 0 and not (isinstance(r, int) and r == 0):
                        rz_low(r, par, 1)
                    if rows:
                        if s == 0:
                            for k in range(KD):
                                rows_sum(r - 1, 1 - par, k)
                        elif s in rows_stage:
                            rows_stage[s](r - 1)
                    elif s == BS - 1:
                        modulation()
                    if ahead and s == 4:
                        nb_low(r + 1, 1 - par)
                    if ahead and s == 6:
                        rz_low(r + 1, 1 - par, 0)

            rows_stage = {2: rows_stats, 4: rows_norm, 5: rows_scale, 6: rows_shift}
            gru_block(0, 0, False, True)
            with dve.Fori(1, NBL - 2, 2) as r:
                gru_block(r, 1, True, True)
                gru_block(r + 1, 0, True, True)
            gru_block(NBL - 1, 1, True, False)
            for k in range(KD):
                rows_sum(NBL - 1, 1, k)
            for s in rows_stage:
                rows_stage[s](NBL - 1)

            def norm_stats(g, base=6):
                dve.wait_ge(ln_T, g + 1)
                for j in range(QUAD):
                    at = j % 2 * D
                    nc.vector.bn_stats(st6[:, j, :], bank[base + j // 2][:, at:at + D]).then_inc(ln_st, 1)
                dve.wait_ge(ln_st, g * QUAD + QUAD)
                even_mean, even_m2, odd_mean, odd_m2 = (st6[:, :, i] for i in (1, 2, 4, 5))
                tt(part[:, 0, :], even_mean, odd_mean, ALU.add).then_inc(ln_ag, 1)
                tt(part[:, 1, :], even_mean, odd_mean, ALU.subtract).then_inc(ln_ag, 1)
                tt(part[:, 2, :], even_m2, odd_m2, ALU.add).then_inc(ln_ag, 1)
                dve.wait_ge(ln_ag, g * 6 + 3)
                ts(mean[:, :], part[:, 0, :], 0.5, None, ALU.mult).then_inc(ln_ag, 1)
                stt(msq[:, :], part[:, 1, :], 0.25, part[:, 1, :], ALU.mult, ALU.mult).then_inc(ln_ag, 1)
                ts(mvar[:, :], part[:, 2, :], 1.0 / D, EPS, ALU.mult, ALU.add).then_inc(ln_ag, 1)
                dve.wait_ge(ln_ag, g * 6 + 6)
                tt(veps[:, :], msq[:, :], mvar[:, :], ALU.add).then_inc(ln_ve, 1)

            def norm_scale(g, base=6):
                dve.wait_ge(ln_rstd, g + 1)
                for j in range(QUAD):
                    at = j % 2 * D
                    op = ts(xn[:, j, :], bank[base + j // 2][:, at:at + D], mean[:, j:j + 1], rstd[:, j:j + 1],
                            ALU.subtract, ALU.mult)
                op.then_inc(ln_xn, 1)

            def norm_modulate(g, base=6):
                dve.wait_ge(ln_B, g + 1)
                if not (isinstance(g, int) and g == 0):
                    dve.wait_ge(ln_lo, g)
                for i in range(QUAD * KD):
                    j, k = i // KD, i % KD
                    at, b = (j % 2 * KD + k) * P, cols(g * QUAD + j, 1)
                    op = ts(yf[:, j, k, :], bank[base + j // 2][:, at:at + P], ada[:, SC2 + k, b], ada[:, SH2 + k, b],
                            ALU.mult, ALU.add)
                op.then_inc(ln_y, 1)

            def step(g, i, u, new=True, soft=True, old=None):
                done = g * H + i
                if soft:
                    dve.wait_ge(s_mm, done)
                    nc.vector.reduce_max(mx[:, :], bank[3][:, :].rearrange("p (j s) -> p j s", j=QUAD),
                                         AX.X).then_inc(s_mx, 1)
                    dve.wait_ge(s_mx, done)
                    nc.vector.tensor_scalar_mul(nmx[:, :], mx[:, :], -SCALE).then_inc(s_nm, 1)
                    dve.wait_ge(v_h, done)
                    tt(v_lo[:, 1 - u, :], bank[2][:, :], v_hi[:, 1 - u, :], ALU.subtract).then_inc(v_l, 1)
                if old is not None:
                    dve.wait_ge(p_h, done - 1)
                    tt(pT_lo[:, :], bank[4][:, :], pT_hi[:, :], ALU.subtract).then_inc(p_l, 1)
                if soft:
                    dve.wait_ge(s_exp, done)
                    nc.vector.reciprocal(rden[:, :], den[:, :]).then_inc(s_rd, 1)
                    dve.wait_ge(s_rd, done)
                    tt(pn[:, 1 - u, :, :], prob[:, :, :], rden[:, :].unsqueeze(2).broadcast_to([P, QUAD, T]),
                       ALU.mult).then_inc(s_pn, 1)
                if new:
                    dve.wait_ge(q_h, done + 1)
                    stt(qT_lo[:, :], bank[0][:, :], bT[:, cols(i + BQ, 1)], qT_hi[:, :], ALU.add,
                        ALU.subtract).then_inc(q_l, 1)
                    dve.wait_ge(k_h, done + 1)
                    stt(kT_lo[:, :], bank[1][:, :], bT[:, cols(i + BQ + H, 1)], kT_hi[:, :], ALU.add,
                        ALU.subtract).then_inc(k_l, 1)
                if old is not None:
                    dve.wait_ge(a_h, done - 1)
                    stt(aT_lo[:, :], bank[5][:, :], bT[:, cols(old, 1)], aT_hi[:, :], ALU.add,
                        ALU.subtract).then_inc(a_l, 1)

            def middle(g):
                step(g, LAG, LAG % 2, old=BV + LAG - 2)
                with dve.Fori(LAG + 1, H - 1, 2) as i:
                    for u in (0, 1):
                        step(g, i + u, u, old=i + (BV + u - 2))

            def residual(g):
                quad = cols(g * QUAD, QUAD)
                dve.wait_ge(o_gated, g + 1)
                for k in range(KD):
                    op = tt(xr2[:, k, quad, :], gated[:, k, :, :], xr[:, k, quad, :], ALU.add)
                op.then_inc(o_res, 1)

            for i in range(LAG):
                step(0, i, i % 2, soft=i >= 1, old=BV + i - 2 if i >= 2 else None)
            with dve.Fori(0, NG - 1) as g:
                middle(g)
                for i in range(LAG):
                    step(g + 1, i, i % 2, old=BV + (i - 2) % H)
                residual(g)
            middle(NG - 1)
            step(NG - 1, H, 0, new=False, old=BV + H - 2)
            norm_stats(0, 0)
            step(NG - 1, H + 1, 1, new=False, soft=False, old=BV + H - 1)
            norm_scale(0, 0)
            norm_modulate(0, 0)
            residual(NG - 1)

            def feed_forward(g, m):
                dve.wait_ge(f_hi, g * FM + (m + 1))
                tt(hid_lo[:, m % 2, :], hf[:, m % 2, :], hid_hi[:, m % 2, :], ALU.subtract).then_inc(f_lo, 1)

            def sum_group(g):
                dve.wait_ge(f_down, g * FM + FM)
                dve.wait_ge(rest_ok, g + 1)
                for j in range(QUAD):
                    b = cols(g * QUAD + j, 1)
                    for k in range(KD):
                        op = stt(yT[:, k, j, :], bank[4 + k][:, j * T:(j + 1) * T], ada[:, G2 + k, b],
                                 xr[:, k, b, :].rearrange("p b t -> p (b t)"), ALU.mult, ALU.add)
                    op.then_inc(f_out, 1)

            for m in range(EARLY):
                feed_forward(0, m)
            with dve.Fori(0, NG - 1) as g:
                for m in range(EARLY, FM):
                    feed_forward(g, m)
                    if m == EARLY:
                        norm_stats(g + 1)
                    elif m == EARLY + 1:
                        norm_scale(g + 1)
                    elif m == EARLY + 3:
                        norm_modulate(g + 1)
                sum_group(g)
                for m in range(EARLY):
                    feed_forward(g + 1, m)
            for m in range(EARLY, FM):
                feed_forward(NG - 1, m)
            sum_group(NG - 1)


_INS = ["x", "cond_2048", "L0_cond_W_ih", "L0_cond_W_hh", "L0_cond_b_ih", "L0_cond_b_hh", "L1_cond_ada_w",
        "L1_cond_ada_b", "L1_cond_qkv_w", "L1_cond_qkv_b", "L1_cond_out_w", "L1_cond_out_b", "L1_cond_ffn_w1",
        "L1_cond_ffn_b1", "L1_cond_ffn_w2", "L1_cond_ffn_b2"]


def kernel(**inputs):
    import numpy as _np
    import concourse.bacc as _bacc
    from concourse.bass_utils import run_bass_kernel_spmd as _run

    nc = _bacc.Bacc("TRN2", target_bir_lowering=False, num_devices=1)
    arrays, args = {}, []
    for name in _INS:
        a = _np.ascontiguousarray(inputs[name])
        arrays[f"in_{name}"] = a
        args.append(nc.dram_tensor(f"in_{name}", a.shape, mybir.dt.from_np(a.dtype), kind="ExternalInput").ap())
    args.append(nc.dram_tensor("out", (B, T, D), mybir.dt.float32, kind="ExternalOutput").ap())
    build(nc, *args)
    r = _run(nc, [arrays], core_ids=[0])
    return r.results[0]["out"]
```

```python
import concourse.bass as bass
from concourse import mybir
from contextlib import ExitStack
import math

P = 128
B, T, D = 16, 128, 256
KD = D // P
GATES = 3 * D
GM = GATES // P
H, DH = 16, 128
INNER = H * DH
MLP = 4 * D
FM = MLP // P
ADA = 6 * D // P
QUAD = 4
NG = B // QUAD
N = QUAD * T
BS = 8
NBL = T // BS
GB = KD * B
assert BS * B == P
EPS = 1e-6
SCALE = DH ** -0.5
CH = 1536
PIECE = CH // 3
WCOLS = (3 * INNER * KD + H * D + KD * MLP + FM * D)
NC = -(-WCOLS // CH)
assert NC == NBL - 2

NORM_END = 12
LAG = 3
EARLY = 2

BI, BH, BA, BQ = 0, GM, 2 * GM, 2 * GM + ADA
BV = BQ + 2 * H
BO = BQ + 3 * H
B1 = BO + KD
B2 = B1 + FM
NB = B2 + KD
SH1, SC1, G1, SH2, SC2, G2 = (i * KD for i in range(6))


def build(nc, x, cond, W_ih, W_hh, b_ih, b_hh, ada_w, ada_b, qkv_w, qkv_b, out_w, out_b,
          f1_w, f1_b, f2_w, f2_b, out):
    f32, f16 = mybir.dt.float32, mybir.dt.float16
    ALU, ACT, AX = mybir.AluOpType, mybir.ActivationFunctionType, mybir.AxisListType
    ctx = ExitStack()
    with ctx:
        def sb(name, shape, dt=f32, scope=ctx):
            return scope.enter_context(nc.sbuf_tensor(name, shape, dt))

        def sem(name):
            return ctx.enter_context(nc.semaphore(name))

        ident = sb("ident", [P, P])
        ident16 = sb("ident16", [P, P], f16)
        w_hi = sb("w_hi", [P, NC * CH], f16)
        w_lo = sb("w_lo", [P, NC * CH], f16)
        bT = sb("bT", [P, NB])
        ada = sb("ada", [P, ADA, B])
        gbo = sb("gbo", [P, KD, B])
        gb2 = sb("gb2", [P, KD, B])
        xr = sb("xr", [P, KD, B, T])
        y_hi = sb("y_hi", [P, KD, B, T], f16)
        y_lo = sb("y_lo", [P, KD, B, T], f16)
        nhalf = sb("nhalf", [P, 8])
        gru = ExitStack()
        stage = sb("stage", [P, 2, CH], f32, gru)
        wg32 = sb("wg32", [P, 2, KD, GATES], f32, gru)
        adaw = sb("adaw", [P, KD, 6 * D], f32, gru)
        brow = sb("brow", [NB, P], f32, gru)
        crow = sb("crow", [B, D], f32, gru)
        whh_hi = sb("whh_hi", [P, KD, GATES], f16, gru)
        whh_lo = sb("whh_lo", [P, KD, GATES], f16, gru)
        wih_hi = sb("wih_hi", [P, KD, GATES], f16, gru)
        wih_lo = sb("wih_lo", [P, KD, GATES], f16, gru)
        bx32 = sb("bx32", [P, BS * GM * B], f32, gru)
        bx_hi = sb("bx_hi", [P, BS * GM * B], f16, gru)
        bx_lo = sb("bx_lo", [P, BS * GM * B], f16, gru)
        bx = sb("bx", [P, GM], f32, gru)
        bn32 = sb("bn32", [P, 2, BS, KD, B], f32, gru)
        condT = sb("condT", [P, KD, B], f32, gru)
        xin = sb("xin", [P, D], f32, gru)
        x32 = sb("x32", [P, 2, KD, P], f32, gru)
        xb_hi = sb("xb_hi", [P, KD, P], f16, gru)
        xb_lo = sb("xb_lo", [P, KD, P], f16, gru)
        grz = [sb(f"grz{i}", [P, 2, BS, 2 * GB], f16, gru) for i in (0, 1)]
        gnb = [sb(f"gnb{i}", [P, 2, BS, GB, 2], f16, gru) for i in (0, 1)]
        hs = sb("hs", [P, 2, BS, GB, 2], f32, gru)
        h_hi = sb("h_hi", [P, GB, 2], f16, gru)
        h_lo = sb("h_lo", [P, GB], f16, gru)
        zr = sb("zr", [P, GB, 2], f32, gru)
        zz = sb("zz", [P, GB, 2], f32, gru)
        nu = sb("nu", [P, GB, 2], f32, gru)
        zg = sb("zg", [P, GB], f32, gru)
        npre = sb("npre", [P, GB, 2], f32, gru)
        xrb = sb("xrb", [P, KD, P], f32, gru)
        natb = sb("natb", [P, D], f32, gru)
        stb = sb("stb", [P, 6], f32, gru)
        lb = sb("lb", [P, 8], f32, gru)
        xnb = sb("xnb", [P, D], f32, gru)
        ym = sb("ym", [P, KD, P], f32, gru)
        yb = sb("yb", [P, KD, P], f32, gru)
        gru.close()
        xr2 = sb("xr2", [P, KD, B, T])
        st6 = sb("st6", [P, QUAD, 6])
        part = sb("part", [P, 3, QUAD])
        mean = sb("mean", [P, QUAD])
        msq = sb("msq", [P, QUAD])
        mvar = sb("mvar", [P, QUAD])
        rstd = sb("rstd", [P, QUAD])
        veps = sb("veps", [P, QUAD])
        tin = sb("tin", [P, QUAD, KD, T])
        nat0 = sb("nat0", [P, QUAD, D])
        xn = sb("xn", [P, QUAD, D])
        yf = sb("yf", [P, QUAD, KD, T])
        qT_hi = sb("qT_hi", [P, N], f16)
        qT_lo = sb("qT_lo", [P, N], f16)
        kT_hi = sb("kT_hi", [P, N], f16)
        kT_lo = sb("kT_lo", [P, N], f16)
        v_hi = sb("v_hi", [P, 2, N], f16)
        v_lo = sb("v_lo", [P, 2, N], f16)
        pT_hi = sb("pT_hi", [P, N], f16)
        pT_lo = sb("pT_lo", [P, N], f16)
        aT_hi = sb("aT_hi", [P, N], f16)
        aT_lo = sb("aT_lo", [P, N], f16)
        prob = sb("prob", [P, QUAD, T])
        pn = sb("pn", [P, 2, QUAD, T])
        mx = sb("mx", [P, QUAD])
        nmx = sb("nmx", [P, QUAD])
        den = sb("den", [P, QUAD])
        rden = sb("rden", [P, QUAD])
        gated = sb("gated", [P, KD, QUAD, T])
        hf = sb("hf", [P, 2, N])
        hid_hi = sb("hid_hi", [P, 2, N], f16)
        hid_lo = sb("hid_lo", [P, 2, N], f16)
        yT = sb("yT", [P, KD, QUAD, T])
        ynat = sb("ynat", [P, B, D])

        bank = [ctx.enter_context(nc.psum_tensor(f"bank{i}", [P, 512], f32)) for i in range(8)]

        AT_O = KD * 3 * INNER
        AT_1 = AT_O + H * D
        AT_2 = AT_1 + KD * MLP
        wq_hi, wq_lo = (w[:, 0:AT_O].rearrange("p (k c) -> p k c", k=KD) for w in (w_hi, w_lo))
        wo_hi, wo_lo = (w[:, AT_O:AT_1] for w in (w_hi, w_lo))
        w1_hi, w1_lo = (w[:, AT_1:AT_2].rearrange("p (k c) -> p k c", k=KD) for w in (w_hi, w_lo))
        w2_hi, w2_lo = (w[:, AT_2:WCOLS].rearrange("p (m c) -> p m c", m=FM) for w in (w_hi, w_lo))

        def sems(names):
            return [sem(n) for n in names.split()]

        stage_in = sems("stage_in0 stage_in1")
        (rows_in, gatew_in, x_in, adaw_in, ident0, ident_ok, const_ok, small_T, small_sb, cond_ok, state_ok,
         wg_hi, wg_lo, ada_mm, ada_add, ada_ok, bx_a, bx_b, bx_c, bx_ok, bn_a, bn_ok, chunk_hi, chunk_lo) = sems(
             "rows_in gatew_in x_in adaw_in ident0 ident_ok const_ok small_T small_sb cond_ok state_ok "
             "wg_hi wg_lo ada_mm ada_add ada_ok bx_a bx_b bx_c bx_ok bn_a bn_ok chunk_hi chunk_lo")
        (r_mm, hn_mm, z_mm, r_ok, z_ok, oz_ok, n_ok, npre_ok, u_ok, hhi_ok, h32_ok, hlo_ok) = sems(
            "r_mm hn_mm z_mm r_ok z_ok oz_ok n_ok npre_ok u_ok hhi_ok h32_ok hlo_ok")
        xt_T, xt_32, xt_hi, xt_lo, rz_mm, nb_mm, rz_hi, nb_hi, rz_lo, nb_lo = sems(
            "xt_T xt_32 xt_hi xt_lo rz_mm nb_mm rz_hi nb_hi rz_lo nb_lo")
        xrb_ok, xr_ok, lb_T, lb_nat, lb_st, lb_a, lb_b, lb_c, lb_r, lb_xn, lb_B, lb_m, lb_y, lb_hi, lb_lo = sems(
            "xrb_ok xr_ok lb_T lb_nat lb_st lb_a lb_b lb_c lb_r lb_xn lb_B lb_m lb_y lb_hi lb_lo")
        (ln_in, ln_ag, ln_p, ln_nat, ln_T, ln_st, ln_ve, ln_rstd, ln_xn, ln_B, ln_y, ln_hi, ln_lo) = sems(
            "ln_in ln_ag ln_p ln_nat ln_T ln_st ln_ve ln_rstd ln_xn ln_B ln_y ln_hi ln_lo")
        (q_mm, k_mm, v_mm, s_mm, p_T, a_mm, o_mm, q_h, k_h, v_h, q_l, k_l, v_l, s_mx, s_nm, s_exp, s_rd, s_pn,
         p_h, p_l, a_h, a_l, o_gated, o_res) = sems(
             "q_mm k_mm v_mm s_mm p_T a_mm o_mm q_h k_h v_h q_l k_l v_l s_mx s_nm s_exp s_rd s_pn "
             "p_h p_l a_h a_l o_gated o_res")
        (f_up, f_gelu, f_hi, f_lo, f_down, rest_a, rest_ok, f_out, y_T, y_nat) = sems(
            "f_up f_gelu f_hi f_lo f_down rest_a rest_ok f_out y_T y_nat")
        y_out = sem("y_out")

        block = ctx.enter_context(nc.Block())

        qkv_v = qkv_w.rearrange("(k p) c -> p k c", p=P)
        wo_v = out_w.rearrange("(h p) d -> p h d", p=P)
        w1_v = f1_w.rearrange("(k p) c -> p k c", p=P)
        w2_v = f2_w.rearrange("(m p) d -> p m d", p=P)
        per_k, half, heads = 3 * INNER // CH, CH // 2, CH // D
        chunks = [[(half * i, qkv_v[:, c // per_k, (c % per_k) * CH + half * i:(c % per_k) * CH + half * (i + 1)])
                   for i in (0, 1)] for c in range(KD * per_k)]
        chunks += [[(half * i, wo_v[:, heads * c + heads // 2 * i:heads * c + heads // 2 * (i + 1), :]) for i in (0, 1)]
                   for c in (0, 1)]
        chunks += [[(0, wo_v[:, 2 * heads:H, :]), (2 * PIECE, w1_v[:, 0, 0:PIECE])],
                   [(0, w1_v[:, 0, PIECE:MLP]), (PIECE, w1_v[:, 1, :])],
                   [(0, w2_v[:, 0:3, :]), (half, w2_v[:, 3:6, :])],
                   [(0, w2_v[:, 6, :]), (D, w2_v[:, 7, :])]]
        assert len(chunks) == NC

        def cols(at, n):
            return slice(at, at + n) if isinstance(at, int) else bass.ds(at, n)

        @block.sync
        def _(sp):
            for at, src, n in ((BI, b_ih, GM), (BH, b_hh, GM), (BA, ada_b, ADA), (BQ, qkv_b, 3 * H), (BO, out_b, KD),
                               (B1, f1_b, FM), (B2, f2_b, KD)):
                sp.dma_start(brow[at:at + n, :], src.rearrange("(n p) -> n p", p=P)).then_inc(rows_in, 16)
            sp.dma_start(crow[:, :], cond).then_inc(rows_in, 16)
            for n, w in enumerate((W_ih, W_hh)):
                sp.dma_start(wg32[:, n, :, :], w.rearrange("(k p) c -> p k c", p=P)).then_inc(gatew_in, 16)

            def load_x(n):
                for t in range(BS):
                    sp.dma_start(xin[t * B:(t + 1) * B, :], x[:, n * BS + t, :]).then_inc(x_in, 16)

            def load_chunk(c):
                if c >= 2:
                    sp.wait_ge(chunk_lo, 3 * (c - 1))
                for at, src in chunks[c]:
                    n = math.prod(src.shape[1:])
                    dst = stage[:, c % 2, at:at + n]
                    sp.dma_start(dst if len(src.shape) == 2 else dst.rearrange("p (a b) -> p a b", a=src.shape[1]),
                                 src).then_inc(stage_in[c % 2], 16)

            load_x(0)
            sp.dma_start(adaw[:, :, :], ada_w.rearrange("(k p) c -> p k c", p=P)).then_inc(adaw_in, 16)
            for c in (0, 1):
                load_chunk(c)
            for n in range(1, NBL):
                sp.wait_ge(xt_T, n)
                load_x(n)
                if 3 <= n <= NC:
                    load_chunk(n - 1)
            out_v = out.rearrange("b t d -> t b d")
            with sp.Fori(0, NG - 1) as g:
                sp.wait_ge(y_nat, g * QUAD + QUAD)
                quad = cols(g * QUAD, QUAD)
                sp.dma_start(out_v[:, quad, :], ynat[:, quad, :]).then_inc(y_out, 16)
            for b in range(B - QUAD, B):
                sp.wait_ge(y_nat, b + 1)
                sp.dma_start(out_v[:, b, :], ynat[:, b, :]).then_inc(y_out, 16)
            sp.wait_ge(y_out, 16 * (NG - 1 + QUAD))

        @block.gpsimd
        def _(pool):
            nc.gpsimd.memset(ident[:, :], 0.0).then_inc(ident0, 1)
            pool.wait_ge(ident0, 1)
            nc.gpsimd.affine_select(out=ident[:, :], in_=ident[:, :], compare_op=ALU.not_equal, fill=1.0, base=0,
                                    pattern=[[-1, P]], channel_multiplier=1).then_inc(ident_ok, 1)
            pool.wait_ge(ident_ok, 1)
            nc.gpsimd.tensor_copy(ident16[:, :], ident[:, :]).then_inc(const_ok, 1)
            nc.gpsimd.memset(nhalf[:, :], -0.5).then_inc(const_ok, 1)
            mul, add, sub = ALU.mult, ALU.add, ALU.subtract
            gtt, gts = nc.gpsimd.tensor_tensor, nc.gpsimd.tensor_scalar

            def x_low(n, par):
                pool.wait_ge(xt_hi, n + 1)
                pool.wait_ge(xt_32, n + 1)
                gtt(xb_lo[:, :, :], x32[:, par, :, :], xb_hi[:, :, :], sub).then_inc(xt_lo, 1)

            def keep_rows(n):
                pool.wait_ge(xrb_ok, n * KD + KD)
                nc.gpsimd.tensor_copy(xr[:, :, :, cols(n * BS, BS)].rearrange("p k b t -> p k t b"),
                                      xrb[:, :, :].rearrange("p k (t b) -> p k t b", b=B)).then_inc(xr_ok, 1)

            def row_stats(n):
                even_mean, even_m2, odd_mean, odd_m2 = (stb[:, i:i + 1] for i in (1, 2, 4, 5))
                pool.wait_ge(lb_st, n + 1)
                gtt(lb[:, 0:1], even_mean, odd_mean, add)
                gtt(lb[:, 1:2], even_mean, odd_mean, sub)
                gtt(lb[:, 2:3], even_m2, odd_m2, add).then_inc(lb_a, 1)
                pool.wait_ge(lb_a, n + 1)
                gtt(lb[:, 4:5], lb[:, 1:2], nhalf[:, 0:1], mul)
                gts(lb[:, 3:4], lb[:, 0:1], 0.5, None, mul)
                gts(lb[:, 5:6], lb[:, 2:3], 1.0 / D, EPS, mul, add).then_inc(lb_b, 1)
                pool.wait_ge(lb_b, n + 1)
                gtt(lb[:, 4:5], lb[:, 4:5], lb[:, 4:5], mul).then_inc(lb_c, 1)
                pool.wait_ge(lb_c, n * 2 + 1)
                gtt(lb[:, 6:7], lb[:, 4:5], lb[:, 5:6], add).then_inc(lb_c, 1)
                pool.wait_ge(lb_c, n * 2 + 2)
                gtt(lb[:, 7:8], lb[:, 6:7], nhalf[:, 0:1], ALU.pow).then_inc(lb_r, 1)

            def y_low(n):
                pool.wait_ge(lb_hi, n + 1)
                at = cols(n * BS, BS)
                gtt(y_lo[:, :, :, at].rearrange("p k b t -> p k t b"),
                    yb[:, :, :].rearrange("p k (t b) -> p k t b", b=B),
                    y_hi[:, :, :, at].rearrange("p k b t -> p k t b"), sub).then_inc(lb_lo, 1)

            def split_chunk(c, par):
                for i in range(3):
                    at = cols(c * CH + i * PIECE, PIECE)
                    pool.wait_ge(chunk_hi, c * 3 + (i + 1))
                    gtt(w_lo[:, at], stage[:, par, i * PIECE:(i + 1) * PIECE], w_hi[:, at], sub).then_inc(chunk_lo, 1)

            def gru_block(r, par):
                x_low(r + 1, 1 - par)
                keep_rows(r - 1)
                row_stats(r - 1)
                split_chunk(r - 1, 1 - par)
                y_low(r - 1)

            nc.gpsimd.memset(lb[:, 0:1], 0.0).then_inc(xr_ok, 1)
            nc.gpsimd.memset(lb[:, 1:2], 0.0).then_inc(lb_lo, 1)
            pool.wait_ge(const_ok, 2)
            x_low(0, 0)
            x_low(1, 1)
            with pool.Fori(1, NBL - 2, 2) as r:
                gru_block(r, 1)
                gru_block(r + 1, 0)
            keep_rows(NBL - 2)
            row_stats(NBL - 2)
            y_low(NBL - 2)
            keep_rows(NBL - 1)
            row_stats(NBL - 1)

            def norm_in(g):
                pool.wait_ge(o_res, g + 1)
                if not (isinstance(g, int) and g == 0):
                    pool.wait_ge(ln_T, g)
                nc.gpsimd.tensor_copy(tin[:, :, :, :].rearrange("p j k t -> p k j t"),
                                      xr2[:, :, cols(g * QUAD, QUAD), :]).then_inc(ln_in, 1)

            def norm_rstd(g):
                pool.wait_ge(ln_ve, g + 1)
                gtt(rstd[:, :], veps[:, :], nhalf[:, 0:QUAD], ALU.pow).then_inc(ln_rstd, 1)

            def norm_low(g):
                pool.wait_ge(ln_hi, g + 1)
                quad = cols(g * QUAD, QUAD)
                gtt(y_lo[:, :, quad, :].rearrange("p k j t -> p j k t"), yf[:, :, :, :],
                    y_hi[:, :, quad, :].rearrange("p k j t -> p j k t"), sub).then_inc(ln_lo, 1)

            def sum_rest(g):
                quad = cols(g * QUAD, QUAD)
                pool.wait_ge(o_res, g + 1)
                for k in range(KD):
                    gtt(xr[:, k, quad, :], xr[:, k, quad, :],
                        gb2[:, k, quad].unsqueeze(2).broadcast_to([P, QUAD, T]), add).then_inc(rest_a, 1)
                pool.wait_ge(rest_a, g * KD + KD)
                gtt(xr[:, :, quad, :], xr[:, :, quad, :], xr2[:, :, quad, :], add).then_inc(rest_ok, 1)

            norm_in(0)
            with pool.Fori(0, NG - 1) as g:
                sum_rest(g)
            with pool.Fori(0, NG - 1) as g:
                norm_rstd(g)
                norm_in(g + 1)
                norm_low(g)
            norm_rstd(NG - 1)
            norm_low(NG - 1)
            sum_rest(NG - 1)

        @block.tensor
        def _(pe):
            def product(ps, w, a, start, stop):
                mm = nc.tensor.matmul
                mm(ps, w[0], a[0], start=start, stop=False, skip_group_check=True)
                mm(ps, w[1], a[0], start=False, stop=False, skip_group_check=True)
                return mm(ps, w[0], a[1], start=False, stop=stop, skip_group_check=True)

            def x_block_T(n):
                pe.wait_ge(x_in, (n + 1) * (16 * BS))
                if not (isinstance(n, int) and n == 0):
                    pe.wait_ge(xt_hi, n)
                    pe.wait_ge(xt_32, n)
                for k in range(KD):
                    mm = nc.tensor.transpose(bank[1][:, k * P:(k + 1) * P], xin[:, k * P:(k + 1) * P], ident[:, :])
                mm.then_inc(xt_T, 1)

            def x_bias(n, rz):
                cut = BS * 2 * GB
                ps, at, last_read = (bank[2], slice(0, cut), rz_lo) if rz else (bank[3], slice(cut, None), nb_lo)
                if not (isinstance(n, int) and n == 0):
                    pe.wait_ge(last_read, 2 * n if rz else n)
                for half, first in ((bx_hi, True), (bx_lo, False)):
                    nc.tensor.matmul(ps[:, 0:cut if rz else cut // 2], ident16[:, :], half[:, at], start=first,
                                     stop=False, skip_group_check=True)

            def x_tile(n, m):
                if m == (0 if isinstance(n, int) and n == 0 else 4):
                    pe.wait_ge(xt_lo, n + 1)
                ps, i, width = (bank[2], m, 4 * B) if m < 4 else (bank[3], m - 4, 2 * B)
                ps = ps[:, 0:BS * width].rearrange("p (t c) -> p t c", c=width)[:, :, i * B:(i + 1) * B]
                w = slice(m * P, (m + 1) * P)
                for k in range(KD):
                    mm = product(ps, (wih_hi[:, k, w], wih_lo[:, k, w]), (xb_hi[:, k, :], xb_lo[:, k, :]), False,
                                 k == KD - 1)
                if m in (3, 5):
                    mm.then_inc(nb_mm if m == 5 else rz_mm, 1)

            def rows_T(n):
                pe.wait_ge(xrb_ok, (n + 1) * KD)
                for k in range(KD):
                    mm = nc.tensor.transpose(bank[4][:, k * P:(k + 1) * P], xrb[:, k, :], ident[:, :])
                mm.then_inc(lb_T, 1)

            def rows_back(n):
                pe.wait_ge(lb_xn, n + 1)
                for k in range(KD):
                    mm = nc.tensor.transpose(bank[5][:, k * P:(k + 1) * P], xnb[:, k * P:(k + 1) * P], ident[:, :])
                mm.then_inc(lb_B, 1)

            pe.wait_ge(ident_ok, 1)
            pe.wait_ge(rows_in, 16 * 8)
            nc.tensor.transpose(bank[0][:, 0:NB], brow[:, :], ident[0:NB, 0:NB])
            for k in range(KD):
                mm = nc.tensor.transpose(bank[0][:, P + k * B:P + (k + 1) * B], crow[:, k * P:(k + 1) * P],
                                         ident[0:B, 0:B])
            mm.then_inc(small_T, 1)
            x_block_T(0)
            pe.wait_ge(bx_ok, 1)
            pe.wait_ge(const_ok, 1)
            pe.wait_ge(wg_lo, 1)
            x_bias(0, True)
            for m in range(4):
                x_tile(0, m)
            x_bias(0, False)
            pe.wait_ge(wg_lo, 2)
            for m in (4, 5):
                x_tile(0, m)
            pe.wait_ge(wg_lo, 3)

            def modulation(tiles):
                for m in tiles:
                    for k in range(KD):
                        mm = nc.tensor.matmul(bank[5][:, m * B:(m + 1) * B], adaw[:, k, m * P:(m + 1) * P],
                                              condT[:, k, :], start=(k == 0), stop=(k == KD - 1))
                if tiles[-1] == ADA - 1:
                    mm.then_inc(ada_mm, 1)

            pe.wait_ge(adaw_in, 16)
            modulation((0, 1, 2))

            pe.wait_ge(bn_ok, 2)
            rb, hb, zb = bank[0], bank[6], bank[7]
            hb2 = hb[:, 0:2 * GB].rearrange("p (j s) -> p j s", s=2)

            def gru_step(r, par, s):
                t1 = r * BS + (s + 1)
                if s == 0:
                    pe.wait_ge(rz_lo, r * 2 + 1)
                    pe.wait_ge(nb_lo, r + 1)
                if s == BS // 2:
                    pe.wait_ge(rz_lo, r * 2 + 2)
                pe.wait_ge(oz_ok, t1)
                for ps, c in ((rb, 0), (zb, GB)):
                    for i in (0, 1):
                        nc.tensor.matmul(ps[:, 0:GB], ident16[:, :], grz[i][:, par, s, c:c + GB], start=(i == 0),
                                         stop=False, skip_group_check=True)
                pe.wait_ge(npre_ok, t1)
                for i in (0, 1):
                    nc.tensor.matmul(hb[:, 0:2 * GB], ident16[:, :], gnb[i][:, par, s, :, :], start=(i == 0),
                                     stop=False, skip_group_check=True)
                pe.wait_ge(hhi_ok, t1)
                r_sums = (0, lambda m: rb[:, m * B:(m + 1) * B])
                hn_sums = (4, lambda m: hb2[:, m * B:(m + 1) * B, 0])
                z_sums = (2, lambda m: zb[:, m * B:(m + 1) * B])

                def gate(sums, high):
                    m0, out = sums
                    for m in range(2):
                        for k in range(KD):
                            w = slice((m0 + m) * P, (m0 + m + 1) * P)
                            a = h_hi[:, k * B:(k + 1) * B, 1] if high else h_lo[:, k * B:(k + 1) * B]
                            for half in (whh_hi, whh_lo) if high else (whh_hi,):
                                mm = nc.tensor.matmul(out(m), half[:, k, w], a, start=False, stop=not high,
                                                      skip_group_check=True)
                    return mm

                gate(r_sums, True)
                gate(hn_sums, True)
                pe.wait_ge(hlo_ok, t1)
                gate(r_sums, False).then_inc(r_mm, 1)
                gate(hn_sums, False).then_inc(hn_mm, 1)
                gate(z_sums, True)
                gate(z_sums, False).then_inc(z_mm, 1)

            def gru_block(r, par, rows, ahead):
                for s in range(BS):
                    gru_step(r, par, s)
                    if ahead:
                        if s == 0:
                            x_block_T(r + 1)
                            x_bias(r + 1, False)
                        elif s == 1:
                            x_bias(r + 1, True)
                        for m in tiles.get(s, ()):
                            x_tile(r + 1, m)
                    if rows and s == 2:
                        rows_T(r - 1)
                    if rows and s == 5:
                        rows_back(r - 1)
                    if not rows and s < 7:
                        modulation(((3, 4), (5,), (6,), (7,), (8,), (9,), (10, 11))[s])

            tiles = {2: (4,), 3: (5, 0), 4: (1, 2), 5: (3,)}
            gru_block(0, 0, False, True)
            with pe.Fori(1, NBL - 2, 2) as r:
                gru_block(r, 1, True, True)
                gru_block(r + 1, 0, True, True)
            gru_block(NBL - 1, 1, True, False)
            rows_T(NBL - 1)

            def first_head(which, t, start):
                w = slice(which * H * DH, which * H * DH + DH)
                ps = bank[which][:, :].rearrange("p (j t) -> p j t", j=QUAD)[:, :, t]
                for k in range(KD):
                    mm = product(ps, (wq_hi[:, k, w], wq_lo[:, k, w]), (y_hi[:, k, 0:QUAD, t], y_lo[:, k, 0:QUAD, t]),
                                 start and k == 0, k == KD - 1)
                return mm

            before, last = slice(0, T - BS), slice(T - BS, T)
            pe.wait_ge(lb_lo, NBL)
            pe.wait_ge(chunk_lo, NC * 3)
            first_head(0, before, True)
            rows_back(NBL - 1)
            first_head(1, before, True)
            pe.wait_ge(lb_lo, NBL + 1)

            def norm_rows(g):
                pe.wait_ge(ln_in, g + 1)
                pe.wait_ge(ln_y, g)
                for i in range(QUAD * KD):
                    j, k = i // KD, i % KD
                    at = (j % 2 * KD + k) * P
                    mm = nc.tensor.transpose(bank[6 + j // 2][:, at:at + P], tin[:, j, k, :], ident[:, :])
                mm.then_inc(ln_T, 1)

            def norm_back(g):
                pe.wait_ge(ln_xn, g + 1)
                for i in range(QUAD * KD):
                    j, k = i // KD, i % KD
                    at = (j % 2 * KD + k) * P
                    mm = nc.tensor.transpose(bank[6 + j // 2][:, at:at + P], xn[:, j, k * P:(k + 1) * P], ident[:, :])
                mm.then_inc(ln_B, 1)

            def norm_pair(back, pair):
                if back:
                    pe.wait_ge(ln_xn, 1)
                else:
                    pe.wait_ge(ln_in, 1)
                for i in range(2 * KD):
                    j, k = 2 * pair + i // KD, i % KD
                    src = xn[:, j, k * P:(k + 1) * P] if back else tin[:, j, k, :]
                    mm = nc.tensor.transpose(bank[4][:, i * P:(i + 1) * P], src, ident[:, :])
                mm.then_inc(ln_B if back and pair else ln_T if pair else ln_p, 1)

            def project_out(g, head, first, last):
                pe.wait_ge(a_l, g * H + (head + 1))
                for k in range(KD):
                    w = cols(head * D + k * P, P)
                    mm = product(bank[6 + k][:, :], (wo_hi[:, w], wo_lo[:, w]), (aT_hi[:, :], aT_lo[:, :]),
                                 first, last)
                if last:
                    mm.then_inc(o_mm, 1)

            def up(g, m):
                first = isinstance(g, int) and g == 0
                quad = cols(g * QUAD, QUAD)
                if m == 0:
                    pe.wait_ge(ln_lo, g + 1)
                if not (first and m < 2):
                    pe.wait_ge(f_gelu, g * FM + (m - 1))
                w = slice(m * P, (m + 1) * P)
                for k in range(KD):
                    mm = product(bank[m % 2][:, :], (w1_hi[:, k, w], w1_lo[:, k, w]),
                                 (y_hi[:, k, quad, :], y_lo[:, k, quad, :]), k == 0, k == KD - 1)
                mm.then_inc(f_up, 1)

            def down(g, m):
                pe.wait_ge(f_lo, g * FM + (m + 1))
                if m == 0 and not (isinstance(g, int) and g == 0):
                    pe.wait_ge(f_out, g * QUAD)
                for k in range(KD):
                    w, a = slice(k * P, (k + 1) * P), m % 2
                    mm = product(bank[2 + k][:, :], (w2_hi[:, m, w], w2_lo[:, m, w]),
                                 (hid_hi[:, a, :], hid_lo[:, a, :]), m == 0, m == FM - 1)
                mm.then_inc(f_down, 1)

            def step(g, i, u, new=True, old=True, add=None, between=None, after=None):
                done = g * H + i
                some = not (isinstance(done, int) and done == 0)
                quad = cols(g * QUAD, QUAD)
                y = [(y_hi[:, k, quad, :], y_lo[:, k, quad, :]) for k in range(KD)]
                if old:
                    pe.wait_ge(s_pn, done - 1)
                    for j in range(QUAD):
                        mm = nc.tensor.transpose(bank[4][:, j * T:(j + 1) * T], pn[:, u, j, :], ident[:, :])
                    mm.then_inc(p_T, 1)
                if new:
                    if some:
                        pe.wait_ge(q_l, done)
                    for k in range(KD if some else 0):
                        w = cols(i * DH, DH)
                        mm = product(bank[0][:, :], (wq_hi[:, k, w], wq_lo[:, k, w]), y[k], k == 0, k == KD - 1)
                    (mm if some else first_head(0, last, False)).then_inc(q_mm, 1)
                if add:
                    project_out(*add)
                if between:
                    between[0](*between[1:])
                if new:
                    if some:
                        pe.wait_ge(k_l, done)
                    for k in range(KD if some else 0):
                        w = cols((i + H) * DH, DH)
                        mm = product(bank[1][:, :], (wq_hi[:, k, w], wq_lo[:, k, w]), y[k], k == 0, k == KD - 1)
                    (mm if some else first_head(1, last, False)).then_inc(k_mm, 1)
                if old:
                    pe.wait_ge(p_l, done - 1)
                    for j in range(QUAD):
                        c = slice(j * T, (j + 1) * T)
                        mm = product(bank[5][:, c], (v_hi[:, u, c], v_lo[:, u, c]), (pT_hi[:, c], pT_lo[:, c]),
                                     j == 0, True)
                    mm.then_inc(a_mm, 1)
                if after:
                    after[0](*after[1:])
                if new:
                    if some:
                        pe.wait_ge(v_l, done)
                    w = cols((i + 2 * H) * DH, DH)
                    for j in range(QUAD):
                        for k in range(KD):
                            mm = product(bank[2][:, j * DH:(j + 1) * DH],
                                         (y_hi[:, k, g * QUAD + j, :], y_lo[:, k, g * QUAD + j, :]),
                                         (wq_hi[:, k, w], wq_lo[:, k, w]), j == 0 and k == 0, k == KD - 1)
                    mm.then_inc(v_mm, 1)
                    pe.wait_ge(q_l, done + 1)
                    pe.wait_ge(k_l, done + 1)
                    if some:
                        pe.wait_ge(s_exp, done)
                    for j in range(QUAD):
                        c = slice(j * T, (j + 1) * T)
                        mm = product(bank[3][:, c], (qT_hi[:, c], qT_lo[:, c]), (kT_hi[:, c], kT_lo[:, c]),
                                     j == 0, True)
                    mm.then_inc(s_mm, 1)

            def middle(g):
                last = isinstance(g, int)
                for i in range(LAG, NORM_END if last else LAG + 1):
                    if last and i > LAG:
                        pe.wait_ge(ln_nat, sum(LAG + n < i for n in pair_steps))
                    step(g, i, i % 2, add=(g, i - LAG, i == LAG, False),
                         after=(norm_pair,) + pair_steps[i - LAG] if last and i - LAG in pair_steps else None)
                with pe.Fori(NORM_END if last else LAG + 1, H - 1, 2) as i:
                    for u in (0, 1):
                        step(g, i + u, u, add=(g, i + (u - LAG), False, False))

            pair_steps = {0: (False, 0), 1: (False, 1), 4: (True, 0), 5: (True, 1)}
            for i in range(LAG):
                step(0, i, i % 2, old=i >= 2)
            with pe.Fori(0, NG - 1) as g:
                middle(g)
                for i in range(LAG):
                    step(g + 1, i, i % 2, add=(g, H - LAG + i, False, i == LAG - 1))
                pe.wait_ge(o_gated, g + 1)
            middle(NG - 1)
            add = [(NG - 1, H - LAG + i, False, i == LAG - 1) for i in range(LAG)]
            step(NG - 1, H, 0, new=False, add=add[0], between=(up, 0, 0))
            step(NG - 1, H + 1, 1, new=False, add=add[1], between=(up, 0, 1), after=(down, 0, 0))
            step(NG - 1, H + 2, 0, new=False, old=False, add=add[2])

            def rows_out(g):
                for j in range(QUAD):
                    pe.wait_ge(f_out, g * QUAD + (j + 1))
                    for k in range(KD):
                        mm = nc.tensor.transpose(bank[4 + j][:, k * P:(k + 1) * P], yT[:, k, j, :], ident[:, :])
                    mm.then_inc(y_T, 1)

            def tiles_to_end(g, normalise):
                for m in range(EARLY, FM):
                    up(g, m)
                    down(g, m - 1)
                    if normalise and m == EARLY:
                        pe.wait_ge(o_gated, NG)
                        norm_rows(g + 1)
                    if normalise and m == EARLY + 2:
                        norm_back(g + 1)

            with pe.Fori(0, NG - 1) as g:
                tiles_to_end(g, True)
                up(g + 1, 0)
                down(g, FM - 1)
                up(g + 1, 1)
                rows_out(g)
                down(g + 1, 0)
                pe.wait_ge(y_nat, g * QUAD + QUAD)
            tiles_to_end(NG - 1, False)
            down(NG - 1, FM - 1)
            rows_out(NG - 1)

        @block.scalar
        def _(act):
            copy, ident_f = ACT.Copy, ACT.Identity
            def x_full(n, par):
                act.wait_ge(xt_T, n + 1)
                if not (isinstance(n, int) and n < 2):
                    act.wait_ge(xrb_ok, (n - 1) * KD)
                nc.scalar.activation(x32[:, par, :, :], bank[1][:, 0:D].rearrange("p (k c) -> p k c", k=KD),
                                     copy).then_inc(xt_32, 1)

            def x_high(n):
                act.wait_ge(xt_T, n + 1)
                nc.scalar.activation(xb_hi[:, :, :], bank[1][:, 0:D].rearrange("p (k c) -> p k c", k=KD),
                                     copy).then_inc(xt_hi, 1)

            def rz_high(n, par):
                act.wait_ge(rz_mm, n + 1)
                nc.scalar.activation(grz[0][:, par, :, :], bank[2][:, :].rearrange("p (t c) -> p t c", t=BS), copy
                                     ).then_inc(rz_hi, 1)

            def nb_high(n, par):
                act.wait_ge(nb_mm, n + 1)
                nc.scalar.activation(gnb[0][:, par, :, :, 1], bank[3][:, 0:BS * GB].rearrange("p (t c) -> p t c", t=BS),
                                     copy).then_inc(nb_hi, 1)

            def rows_full(n):
                act.wait_ge(lb_T, n + 1)
                nc.scalar.activation(natb[:, :], bank[4][:, 0:D], copy).then_inc(lb_nat, 1)

            def y_high(n):
                act.wait_ge(lb_y, n + 1)
                for k in range(KD):
                    op = nc.scalar.activation(y_hi[:, k, :, cols(n * BS, BS)].rearrange("p b t -> p t b"),
                                              yb[:, k, :].rearrange("p (t b) -> p t b", b=B), copy)
                op.then_inc(lb_hi, 1)

            def piece_high(r, par, i):
                if i == 0:
                    act.wait_ge(stage_in[1 - par], (r + par) * 16)
                nc.scalar.activation(w_hi[:, cols((r - 1) * CH + i * PIECE, PIECE)],
                                     stage[:, 1 - par, i * PIECE:(i + 1) * PIECE], copy).then_inc(chunk_hi, 1)

            act.wait_ge(npre_ok, 1)
            nc.scalar.activation(zg[:, :], zr[:, :, 0], ACT.Sigmoid).then_inc(oz_ok, 1)
            splits = ((wih_hi, 0, slice(0, 2 * D)), (wih_hi, 0, slice(2 * D, 3 * D)), (whh_hi, 1, slice(0, 3 * D)))
            act.wait_ge(gatew_in, 32)
            for hi, n, c in splits[:1]:
                nc.scalar.activation(hi[:, :, c], wg32[:, n, :, c], copy).then_inc(wg_hi, 1)
            x_high(0)
            x_full(0, 0)
            for hi, n, c in splits[1:]:
                nc.scalar.activation(hi[:, :, c], wg32[:, n, :, c], copy).then_inc(wg_hi, 1)
            rz_high(0, 0)
            act.wait_ge(bn_ok, 1)
            nb_high(0, 0)

            def gru_block(r, par, rows, ahead):
                for s in range(BS):
                    t1 = r * BS + (s + 1)
                    act.wait_ge(r_mm, t1)
                    nc.scalar.activation(zr[:, :, 1], bank[0][:, 0:GB], ACT.Sigmoid).then_inc(r_ok, 1)
                    act.wait_ge(z_mm, t1)
                    nc.scalar.activation(zg[:, :], bank[7][:, 0:GB], ACT.Sigmoid).then_inc(z_ok, 1)
                    nc.scalar.activation(zz[:, :, 1], bank[7][:, 0:GB], ACT.Sigmoid, scale=-1.0).then_inc(oz_ok, 1)
                    act.wait_ge(npre_ok, t1 + 1)
                    nc.scalar.activation(nu[:, :, 0], npre[:, :, 1], ACT.Tanh).then_inc(n_ok, 1)
                    if ahead:
                        if s == 0:
                            x_high(r + 1)
                        elif s == 1:
                            x_full(r + 1, 1 - par)
                        elif s == 4:
                            nb_high(r + 1, 1 - par)
                        elif s == 5:
                            rz_high(r + 1, 1 - par)
                    if rows and s == 2:
                        rows_full(r - 1)
                    if rows and ahead and s in (3, 4, 6):
                        piece_high(r, par, {3: 0, 4: 1, 6: 2}[s])
                    if rows and s == 7:
                        y_high(r - 1)

            gru_block(0, 0, False, True)
            with act.Fori(1, NBL - 2, 2) as r:
                gru_block(r, 1, True, True)
                gru_block(r + 1, 0, True, True)
            gru_block(NBL - 1, 1, True, False)
            rows_full(NBL - 1)
            y_high(NBL - 1)

            def norm_high(g):
                act.wait_ge(ln_y, g + 1)
                nc.scalar.activation(y_hi[:, :, cols(g * QUAD, QUAD), :].rearrange("p k j t -> p j k t"),
                                     yf[:, :, :, :], copy).then_inc(ln_hi, 1)

            def gate_out(g):
                act.wait_ge(o_mm, g + 1)
                for k in range(KD):
                    for j in range(QUAD):
                        b = g * QUAD + j
                        op = nc.scalar.activation(gated[:, k, j, :], bank[6 + k][:, j * T:(j + 1) * T], ident_f,
                                                  bias=gbo[:, k, cols(b, 1)], scale=ada[:, G1 + k, cols(b, 1)])
                op.then_inc(o_gated, 1)

            def norm_copy(pair):
                act.wait_ge(*pair_ready[pair])
                nc.scalar.activation(nat0[:, 2 * (pair % 2):2 * (pair % 2) + 2, :],
                                     bank[4][:, :].rearrange("p (j d) -> p j d", j=2), copy).then_inc(ln_nat, 1)

            pair_ready = [(ln_p, 1), (ln_T, 1), (ln_p, 2), (ln_B, 1)]

            def feed_forward(g, m):
                first = isinstance(g, int) and g == 0
                act.wait_ge(f_up, g * FM + (m + 1))
                if not (first and m < 2):
                    act.wait_ge(f_lo, g * FM + (m - 1))
                nc.scalar.activation(hf[:, m % 2, :], bank[m % 2][:, :], ACT.Gelu,
                                     bias=bT[:, B1 + m:B1 + m + 1]).then_inc(f_gelu, 1)
                act.wait_ge(f_gelu, g * FM + (m + 1))
                if not (first and m < 2):
                    act.wait_ge(f_down, g * FM + (m - 1))
                nc.scalar.activation(hid_hi[:, m % 2, :], hf[:, m % 2, :], copy).then_inc(f_hi, 1)

            def step(g, i, u, new=True, soft=True, old=None, gated_group=None, between=None, after=None):
                done = g * H + i
                if old is not None:
                    act.wait_ge(p_T, done - 1)
                    nc.scalar.activation(pT_hi[:, :], bank[4][:, :], copy).then_inc(p_h, 1)
                if soft:
                    act.wait_ge(s_nm, done)
                    if not (isinstance(done, int) and done == 1):
                        act.wait_ge(s_pn, done - 1)
                    for j in range(QUAD):
                        op = nc.scalar.activation(prob[:, j, :], bank[3][:, j * T:(j + 1) * T], ACT.Exp,
                                                  bias=nmx[:, j:j + 1], scale=SCALE, accum_out=den[:, j:j + 1])
                    op.then_inc(s_exp, 1)
                if new:
                    act.wait_ge(q_mm, done + 1)
                    if soft:
                        act.wait_ge(s_mm, done)
                    nc.scalar.activation(qT_hi[:, :], bank[0][:, :], ident_f,
                                         bias=bT[:, cols(i + BQ, 1)]).then_inc(q_h, 1)
                    act.wait_ge(k_mm, done + 1)
                    nc.scalar.activation(kT_hi[:, :], bank[1][:, :], ident_f,
                                         bias=bT[:, cols(i + BQ + H, 1)]).then_inc(k_h, 1)
                if gated_group is not None:
                    gate_out(gated_group)
                if between:
                    between[0](*between[1:])
                if old is not None:
                    act.wait_ge(a_mm, done - 1)
                    nc.scalar.activation(aT_hi[:, :], bank[5][:, :], ident_f,
                                         bias=bT[:, cols(old, 1)]).then_inc(a_h, 1)
                if after:
                    after[0](*after[1:])
                if new:
                    act.wait_ge(v_mm, done + 1)
                    nc.scalar.activation(v_hi[:, u, :], bank[2][:, :], copy).then_inc(v_h, 1)

            def middle(g):
                last = isinstance(g, int)
                for i in range(LAG, NORM_END if last else LAG + 1):
                    step(g, i, i % 2, old=BV + i - 2, after=other[i - LAG] if last and i - LAG in other else None)
                with act.Fori(NORM_END if last else LAG + 1, H - 1, 2) as i:
                    for u in (0, 1):
                        step(g, i + u, u, old=i + (BV + u - 2))

            other = {0: (norm_copy, 0), 1: (norm_copy, 1), 4: (norm_copy, 2), 5: (norm_copy, 3), 8: (norm_high, 0)}
            for i in range(LAG):
                step(0, i, i % 2, soft=i >= 1, old=BV + i - 2 if i >= 2 else None)
            with act.Fori(0, NG - 1) as g:
                middle(g)
                for i in range(LAG):
                    step(g + 1, i, i % 2, old=BV + (i - 2) % H, gated_group=g if i == LAG - 1 else None)
            middle(NG - 1)
            step(NG - 1, H, 0, new=False, old=BV + H - 2, between=(feed_forward, 0, 0))
            step(NG - 1, H + 1, 1, new=False, soft=False, old=BV + H - 1, between=(feed_forward, 0, 1))
            gate_out(NG - 1)

            def rows_out(g):
                for j in range(QUAD):
                    act.wait_ge(y_T, g * QUAD + (j + 1))
                    nc.scalar.activation(ynat[:, cols(g * QUAD + j, 1), :],
                                         bank[4 + j][:, 0:D].unsqueeze(1), copy).then_inc(y_nat, 1)

            with act.Fori(0, NG - 1) as g:
                for m in range(EARLY, FM):
                    feed_forward(g, m)
                    if m == EARLY + 3:
                        norm_high(g + 1)
                for m in range(EARLY):
                    feed_forward(g + 1, m)
                rows_out(g)
            for m in range(EARLY, FM):
                feed_forward(NG - 1, m)
            rows_out(NG - 1)

        @block.vector
        def _(dve):
            tt, ts, stt = nc.vector.tensor_tensor, nc.vector.tensor_scalar, nc.vector.scalar_tensor_tensor
            copy = nc.vector.tensor_copy
            nc.vector.memset(zr[:, :, :], 0.0)
            nc.vector.memset(zz[:, :, :], 0.0)
            nc.vector.memset(npre[:, :, :], 0.0).then_inc(npre_ok, 1)
            dve.wait_ge(npre_ok, 1)
            dve.wait_ge(small_T, 1)
            copy(bT[:, :], bank[0][:, 0:NB]).then_inc(small_sb, 1)
            copy(condT[:, :, :], bank[0][:, P:P + GB].rearrange("p (k b) -> p k b", k=KD)).then_inc(cond_ok, 1)
            dve.wait_ge(small_sb, 1)
            tt(bx[:, 0:4], bT[:, BI:BI + 4], bT[:, BH:BH + 4], ALU.add).then_inc(bx_a, 1)
            copy(bx[:, 4:6], bT[:, BI + 4:BI + 6]).then_inc(bx_a, 1)
            copy(bn32[:, :, :, :, :].rearrange("p r t k b -> p (r t) k b"),
                 bT[:, BH + 4:BH + 6].unsqueeze(1).unsqueeze(3).broadcast_to([P, 2 * BS, KD, B])).then_inc(bn_a, 1)
            dve.wait_ge(bx_a, 2)
            rz = BS * 2 * GB
            for at, n_tiles, m0 in ((0, 4, 0), (rz, 2, 4)):
                copy(bx32[:, at:at + BS * n_tiles * B].rearrange("p (t m b) -> p t m b", t=BS, m=n_tiles),
                     bx[:, m0:m0 + n_tiles].unsqueeze(1).unsqueeze(3).broadcast_to([P, BS, n_tiles, B])
                     ).then_inc(bx_b, 1)
            dve.wait_ge(bn_a, 1)
            bn = bn32[:, :, :, :, :].rearrange("p r t k b -> p (r t k b)")
            nb = [g[:, :, :, :, 0].rearrange("p r t j -> p (r t j)") for g in gnb]
            copy(nb[0], bn).then_inc(bn_ok, 1)
            dve.wait_ge(bx_b, 2)
            copy(bx_hi[:, :], bx32[:, :]).then_inc(bx_c, 1)
            dve.wait_ge(bn_ok, 1)
            tt(nb[1], bn, nb[0], ALU.subtract).then_inc(bn_ok, 1)
            dve.wait_ge(bx_c, 1)
            tt(bx_lo[:, :], bx32[:, :], bx_hi[:, :], ALU.subtract).then_inc(bx_ok, 1)
            dve.wait_ge(cond_ok, 1)
            cond_row = condT[:, :, :].rearrange("p k b -> p (k b)")
            copy(hs[:, 1, BS - 1, :, 1], cond_row).then_inc(state_ok, 1)
            copy(h_hi[:, :, 1], cond_row).then_inc(hhi_ok, 1)
            dve.wait_ge(state_ok, 1)
            dve.wait_ge(hhi_ok, 1)
            tt(h_lo[:, :], cond_row, h_hi[:, :, 1], ALU.subtract).then_inc(hlo_ok, 1)
            for i, (hi, lo, n, c) in enumerate(((wih_hi, wih_lo, 0, slice(0, 2 * D)),
                                                (wih_hi, wih_lo, 0, slice(2 * D, 3 * D)),
                                                (whh_hi, whh_lo, 1, slice(0, 3 * D)))):
                dve.wait_ge(wg_hi, i + 1)
                tt(lo[:, :, c], wg32[:, n, :, c], hi[:, :, c], ALU.subtract).then_inc(wg_lo, 1)
            def modulation():
                dve.wait_ge(ada_mm, 1)
                tt(ada[:, :, :], bank[5][:, 0:ADA * B].rearrange("p (m b) -> p m b", b=B),
                   bT[:, BA:BA + ADA].unsqueeze(2).broadcast_to([P, ADA, B]), ALU.add).then_inc(ada_add, 1)
                dve.wait_ge(ada_add, 1)
                for sc in (SC1, SC2):
                    nc.vector.tensor_scalar_add(ada[:, sc:sc + KD, :], ada[:, sc:sc + KD, :], 1.0).then_inc(ada_ok, 1)
                for dst, gate_tile, bias in ((gbo, G1, BO), (gb2, G2, B2)):
                    tt(dst[:, :, :], ada[:, gate_tile:gate_tile + KD, :],
                       bT[:, bias:bias + KD].unsqueeze(2).broadcast_to([P, KD, B]), ALU.mult).then_inc(ada_ok, 1)

            def rz_low(n, par, half):
                t, c = slice(half * BS // 2, (half + 1) * BS // 2), BS * GB
                if half == 0:
                    dve.wait_ge(rz_hi, n + 1)
                tt(grz[1][:, par, t, :], bank[2][:, half * c:(half + 1) * c].rearrange("p (t c) -> p t c", t=BS // 2),
                   grz[0][:, par, t, :], ALU.subtract).then_inc(rz_lo, 1)

            def nb_low(n, par):
                dve.wait_ge(nb_hi, n + 1)
                tt(gnb[1][:, par, :, :, 1], bank[3][:, 0:BS * GB].rearrange("p (t c) -> p t c", t=BS),
                   gnb[0][:, par, :, :, 1], ALU.subtract).then_inc(nb_lo, 1)

            def rows_sum(n, par, k):
                if k == 0:
                    dve.wait_ge(h32_ok, (n + 1) * BS)
                    dve.wait_ge(xr_ok, n + 1)
                tt(xrb[:, k, :].rearrange("p (t b) -> p t b", b=B),
                   x32[:, par, k, :].rearrange("p (t b) -> p t b", b=B),
                   hs[:, par, :, k * B:(k + 1) * B, 1], ALU.add).then_inc(xrb_ok, 1)

            def rows_stats(n):
                dve.wait_ge(lb_nat, n + 1)
                nc.vector.bn_stats(stb[:, :], natb[:, :]).then_inc(lb_st, 1)

            def rows_norm(n):
                dve.wait_ge(lb_r, n + 1)
                ts(xnb[:, :], natb[:, :], lb[:, 3:4], lb[:, 7:8], ALU.subtract, ALU.mult).then_inc(lb_xn, 1)

            def modulate(dst, src, tile, op, done, n):
                tt(dst[:, :, :].rearrange("p k (t b) -> p k t b", b=B),
                   src.rearrange("p (k t b) -> p k t b", k=KD, b=B),
                   ada[:, tile:tile + KD, :].unsqueeze(2).broadcast_to([P, KD, BS, B]), op).then_inc(done, 1)

            def rows_scale(n):
                dve.wait_ge(lb_B, n + 1)
                dve.wait_ge(ada_ok, 4)
                modulate(ym, bank[5][:, 0:D], SC1, ALU.mult, lb_m, n)

            def rows_shift(n):
                dve.wait_ge(lb_m, n + 1)
                dve.wait_ge(lb_lo, n + 1)
                modulate(yb, ym[:, :, :].rearrange("p k c -> p (k c)"), SH1, ALU.add, lb_y, n)

            for half in (0, 1):
                rz_low(0, 0, half)
            nb_low(0, 0)

            def gru_block(r, par, rows, ahead):
                for s in range(BS):
                    t1 = r * BS + (s + 1)
                    dve.wait_ge(r_ok, t1)
                    dve.wait_ge(hn_mm, t1)
                    nc.vector.tensor_tensor_scan(npre[:, :, :].rearrange("p j s -> p (j s)"),
                                                 zr[:, :, :].rearrange("p j s -> p (j s)"), bank[6][:, 0:2 * GB], 0.0,
                                                 ALU.mult, ALU.add).then_inc(npre_ok, 1)
                    dve.wait_ge(z_ok, t1)
                    before = hs[:, 1 - par, BS - 1, :, 1] if s == 0 else hs[:, par, s - 1, :, 1]
                    tt(nu[:, :, 1], zg[:, :], before, ALU.mult).then_inc(u_ok, 1)
                    dve.wait_ge(u_ok, t1)
                    dve.wait_ge(n_ok, t1)
                    gates = (zz[:, :, :].rearrange("p j s -> p (j s)"), nu[:, :, :].rearrange("p j s -> p (j s)"),
                             0.0, ALU.mult, ALU.add)
                    nc.vector.tensor_tensor_scan(h_hi[:, :, :].rearrange("p j s -> p (j s)"), *gates
                                                 ).then_inc(hhi_ok, 1)
                    nc.vector.tensor_tensor_scan(hs[:, par, s, :, :].rearrange("p j s -> p (j s)"), *gates
                                                 ).then_inc(h32_ok, 1)
                    dve.wait_ge(h32_ok, t1)
                    tt(h_lo[:, :], hs[:, par, s, :, 1], h_hi[:, :, 1], ALU.subtract).then_inc(hlo_ok, 1)
                    if s == 0 and not (isinstance(r, int) and r == 0):
                        rz_low(r, par, 1)
                    if rows:
                        if s == 0:
                            for k in range(KD):
                                rows_sum(r - 1, 1 - par, k)
                        elif s in rows_stage:
                            rows_stage[s](r - 1)
                    elif s == BS - 1:
                        modulation()
                    if ahead and s == 4:
                        nb_low(r + 1, 1 - par)
                    if ahead and s == 6:
                        rz_low(r + 1, 1 - par, 0)

            rows_stage = {2: rows_stats, 4: rows_norm, 5: rows_scale, 6: rows_shift}
            gru_block(0, 0, False, True)
            with dve.Fori(1, NBL - 2, 2) as r:
                gru_block(r, 1, True, True)
                gru_block(r + 1, 0, True, True)
            gru_block(NBL - 1, 1, True, False)
            for k in range(KD):
                rows_sum(NBL - 1, 1, k)
            for s in rows_stage:
                rows_stage[s](NBL - 1)
            dve.wait_ge(lb_hi, NBL)
            last = slice((NBL - 1) * BS, T)
            tt(y_lo[:, :, :, last].rearrange("p k b t -> p k t b"), yb[:, :, :].rearrange("p k (t b) -> p k t b", b=B),
               y_hi[:, :, :, last].rearrange("p k b t -> p k t b"), ALU.subtract).then_inc(lb_lo, 1)

            def rows(g, j):
                return nat0[:, j, :] if isinstance(g, int) else bank[6 + j // 2][:, j % 2 * D:(j % 2 + 1) * D]

            def norm_stats(g):
                if isinstance(g, int):
                    dve.wait_ge(ln_nat, 2)
                dve.wait_ge(ln_T, g + 1)
                for j in range(QUAD):
                    nc.vector.bn_stats(st6[:, j, :], rows(g, j)).then_inc(ln_st, 1)
                dve.wait_ge(ln_st, g * QUAD + QUAD)
                even_mean, even_m2, odd_mean, odd_m2 = (st6[:, :, i] for i in (1, 2, 4, 5))
                tt(part[:, 0, :], even_mean, odd_mean, ALU.add).then_inc(ln_ag, 1)
                tt(part[:, 1, :], even_mean, odd_mean, ALU.subtract).then_inc(ln_ag, 1)
                tt(part[:, 2, :], even_m2, odd_m2, ALU.add).then_inc(ln_ag, 1)
                dve.wait_ge(ln_ag, g * 6 + 3)
                ts(mean[:, :], part[:, 0, :], 0.5, None, ALU.mult).then_inc(ln_ag, 1)
                stt(msq[:, :], part[:, 1, :], 0.25, part[:, 1, :], ALU.mult, ALU.mult).then_inc(ln_ag, 1)
                ts(mvar[:, :], part[:, 2, :], 1.0 / D, EPS, ALU.mult, ALU.add).then_inc(ln_ag, 1)
                dve.wait_ge(ln_ag, g * 6 + 6)
                tt(veps[:, :], msq[:, :], mvar[:, :], ALU.add).then_inc(ln_ve, 1)

            def norm_scale(g):
                dve.wait_ge(ln_rstd, g + 1)
                for j in range(QUAD):
                    op = ts(xn[:, j, :], rows(g, j), mean[:, j:j + 1], rstd[:, j:j + 1],
                            ALU.subtract, ALU.mult)
                op.then_inc(ln_xn, 1)

            def norm_modulate(g, seqs=range(QUAD)):
                if isinstance(g, int):
                    dve.wait_ge(ln_nat, 4)
                else:
                    dve.wait_ge(ln_lo, g)
                dve.wait_ge(ln_B, g + 1)
                for j in seqs:
                    for k in range(KD):
                        b = cols(g * QUAD + j, 1)
                        op = ts(yf[:, j, k, :], rows(g, j)[:, k * P:(k + 1) * P], ada[:, SC2 + k, b],
                                ada[:, SH2 + k, b], ALU.mult, ALU.add)
                if seqs[-1] == QUAD - 1:
                    op.then_inc(ln_y, 1)

            def feed_forward(g, m):
                dve.wait_ge(f_hi, g * FM + (m + 1))
                tt(hid_lo[:, m % 2, :], hf[:, m % 2, :], hid_hi[:, m % 2, :], ALU.subtract).then_inc(f_lo, 1)

            def step(g, i, u, new=True, soft=True, old=None, between=None, after=None):
                done = g * H + i
                if soft:
                    dve.wait_ge(s_mm, done)
                    nc.vector.reduce_max(mx[:, :], bank[3][:, :].rearrange("p (j s) -> p j s", j=QUAD),
                                         AX.X).then_inc(s_mx, 1)
                    dve.wait_ge(s_mx, done)
                    nc.vector.tensor_scalar_mul(nmx[:, :], mx[:, :], -SCALE).then_inc(s_nm, 1)
                    dve.wait_ge(v_h, done)
                    tt(v_lo[:, 1 - u, :], bank[2][:, :], v_hi[:, 1 - u, :], ALU.subtract).then_inc(v_l, 1)
                if old is not None:
                    dve.wait_ge(p_h, done - 1)
                    tt(pT_lo[:, :], bank[4][:, :], pT_hi[:, :], ALU.subtract).then_inc(p_l, 1)
                if soft:
                    dve.wait_ge(s_exp, done)
                    nc.vector.reciprocal(rden[:, :], den[:, :]).then_inc(s_rd, 1)
                    dve.wait_ge(s_rd, done)
                    tt(pn[:, 1 - u, :, :], prob[:, :, :], rden[:, :].unsqueeze(2).broadcast_to([P, QUAD, T]),
                       ALU.mult).then_inc(s_pn, 1)
                if new:
                    dve.wait_ge(q_h, done + 1)
                    stt(qT_lo[:, :], bank[0][:, :], bT[:, cols(i + BQ, 1)], qT_hi[:, :], ALU.add,
                        ALU.subtract).then_inc(q_l, 1)
                    dve.wait_ge(k_h, done + 1)
                    stt(kT_lo[:, :], bank[1][:, :], bT[:, cols(i + BQ + H, 1)], kT_hi[:, :], ALU.add,
                        ALU.subtract).then_inc(k_l, 1)
                if between:
                    between[0](*between[1:])
                if old is not None:
                    dve.wait_ge(a_h, done - 1)
                    stt(aT_lo[:, :], bank[5][:, :], bT[:, cols(old, 1)], aT_hi[:, :], ALU.add,
                        ALU.subtract).then_inc(a_l, 1)
                if after:
                    after[0](*after[1:])

            def middle(g):
                last = isinstance(g, int)
                for i in range(LAG, NORM_END if last else LAG + 1):
                    step(g, i, i % 2, old=BV + i - 2, after=other[i - LAG] if last and i - LAG in other else None)
                with dve.Fori(NORM_END if last else LAG + 1, H - 1, 2) as i:
                    for u in (0, 1):
                        step(g, i + u, u, old=i + (BV + u - 2))

            def residual(g):
                quad = cols(g * QUAD, QUAD)
                dve.wait_ge(o_gated, g + 1)
                for k in range(KD):
                    op = tt(xr2[:, k, quad, :], gated[:, k, :, :], xr[:, k, quad, :], ALU.add)
                op.then_inc(o_res, 1)

            other = {2: (norm_stats, 0), 3: (norm_scale, 0), 6: (norm_modulate, 0, (0, 1)),
                     7: (norm_modulate, 0, (2, 3))}
            for i in range(LAG):
                step(0, i, i % 2, soft=i >= 1, old=BV + i - 2 if i >= 2 else None)
            with dve.Fori(0, NG - 1) as g:
                middle(g)
                for i in range(LAG):
                    step(g + 1, i, i % 2, old=BV + (i - 2) % H)
                residual(g)
            middle(NG - 1)
            step(NG - 1, H, 0, new=False, old=BV + H - 2, between=(feed_forward, 0, 0))
            step(NG - 1, H + 1, 1, new=False, soft=False, old=BV + H - 1, between=(feed_forward, 0, 1))
            residual(NG - 1)

            def sum_group(g):
                dve.wait_ge(f_down, g * FM + FM)
                dve.wait_ge(rest_ok, g + 1)
                for j in range(QUAD):
                    b = cols(g * QUAD + j, 1)
                    for k in range(KD):
                        op = stt(yT[:, k, j, :], bank[2 + k][:, j * T:(j + 1) * T], ada[:, G2 + k, b],
                                 xr[:, k, b, :].rearrange("p b t -> p (b t)"), ALU.mult, ALU.add)
                    op.then_inc(f_out, 1)

            with dve.Fori(0, NG - 1) as g:
                for m in range(EARLY, FM):
                    feed_forward(g, m)
                    if m == EARLY:
                        norm_stats(g + 1)
                    elif m == EARLY + 1:
                        norm_scale(g + 1)
                    elif m == EARLY + 2:
                        norm_modulate(g + 1)
                sum_group(g)
                for m in range(EARLY):
                    feed_forward(g + 1, m)
            for m in range(EARLY, FM):
                feed_forward(NG - 1, m)
            sum_group(NG - 1)


_INS = ["x", "cond_2048", "L0_cond_W_ih", "L0_cond_W_hh", "L0_cond_b_ih", "L0_cond_b_hh", "L1_cond_ada_w",
        "L1_cond_ada_b", "L1_cond_qkv_w", "L1_cond_qkv_b", "L1_cond_out_w", "L1_cond_out_b", "L1_cond_ffn_w1",
        "L1_cond_ffn_b1", "L1_cond_ffn_w2", "L1_cond_ffn_b2"]


def kernel(**inputs):
    import numpy as _np
    import concourse.bacc as _bacc
    from concourse.bass_utils import run_bass_kernel_spmd as _run

    nc = _bacc.Bacc("TRN2", target_bir_lowering=False, num_devices=1)
    arrays, args = {}, []
    for name in _INS:
        a = _np.ascontiguousarray(inputs[name])
        arrays[f"in_{name}"] = a
        args.append(nc.dram_tensor(f"in_{name}", a.shape, mybir.dt.from_np(a.dtype), kind="ExternalInput").ap())
    args.append(nc.dram_tensor("out", (B, T, D), mybir.dt.float32, kind="ExternalOutput").ap())
    build(nc, *args)
    r = _run(nc, [arrays], core_ids=[0])
    return r.results[0]["out"]
```
